# Optimizing a Trainium2 kernel written in Bass

```python
import numpy as np
import jax
import jax.numpy as jnp

def _softmax(x, axis=-1):
    return jax.nn.softmax(x, axis=axis)

def _gelu(x):
    return jax.nn.gelu(x, approximate=True)

def _silu(x):
    return jax.nn.silu(x)

def _sigmoid(x):
    return jax.nn.sigmoid(x)

def _layernorm(x, axis=-1, eps=1e-05):
    m = jnp.mean(x, axis=axis, keepdims=True)
    v = jnp.var(x, axis=axis, keepdims=True)
    return (x - m) / jnp.sqrt(v + eps)

def _scatter_add(tgt, idx, src, axis=0):
    return tgt.at[idx].add(src)

def _segment_sum(src, seg, n):
    return jax.ops.segment_sum(src, seg, n)
kernel_name = 'mk_dlrm_tower_d1_rec_r8_8f77e2'

def setup_inputs(seed: int=0):
    np.random.seed(seed)
    _w = jnp.asarray

    def _rec_inputs():
        import jax
        import jax.numpy as jnp
        _tk = jax.random.key(seed)
        ids = jnp.stack([jax.random.randint(jax.random.fold_in(_tk, 200 + f), (512,), 0, v, jnp.int32) for f, v in enumerate([125000, 12500, 12500, 125000, 1000, 1000, 12500, 1000, 1250, 12500, 12500, 1000, 1000, 12500, 1000, 1250, 1000, 1250, 12500, 1000, 125000, 1250, 12500, 1000, 1250, 1000])], axis=1)
        tbl_0 = 0.05 * jax.random.normal(jax.random.fold_in(_tk, 500 + 0), (125000, 64), jnp.float32)
        tbl_1 = 0.05 * jax.random.normal(jax.random.fold_in(_tk, 500 + 1), (12500, 64), jnp.float32)
        tbl_2 = 0.05 * jax.random.normal(jax.random.fold_in(_tk, 500 + 2), (12500, 64), jnp.float32)
        tbl_3 = 0.05 * jax.random.normal(jax.random.fold_in(_tk, 500 + 3), (125000, 64), jnp.float32)
        tbl_4 = 0.05 * jax.random.normal(jax.random.fold_in(_tk, 500 + 4), (1000, 64), jnp.float32)
        tbl_5 = 0.05 * jax.random.normal(jax.random.fold_in(_tk, 500 + 5), (1000, 64), jnp.float32)
        tbl_6 = 0.05 * jax.random.normal(jax.random.fold_in(_tk, 500 + 6), (12500, 64), jnp.float32)
        tbl_7 = 0.05 * jax.random.normal(jax.random.fold_in(_tk, 500 + 7), (1000, 64), jnp.float32)
        tbl_8 = 0.05 * jax.random.normal(jax.random.fold_in(_tk, 500 + 8), (1250, 64), jnp.float32)
        tbl_9 = 0.05 * jax.random.normal(jax.random.fold_in(_tk, 500 + 9), (12500, 64), jnp.float32)
        tbl_10 = 0.05 * jax.random.normal(jax.random.fold_in(_tk, 500 + 10), (12500, 64), jnp.float32)
        tbl_11 = 0.05 * jax.random.normal(jax.random.fold_in(_tk, 500 + 11), (1000, 64), jnp.float32)
        tbl_12 = 0.05 * jax.random.normal(jax.random.fold_in(_tk, 500 + 12), (1000, 64), jnp.float32)
        tbl_13 = 0.05 * jax.random.normal(jax.random.fold_in(_tk, 500 + 13), (12500, 64), jnp.float32)
        tbl_14 = 0.05 * jax.random.normal(jax.random.fold_in(_tk, 500 + 14), (1000, 64), jnp.float32)
        tbl_15 = 0.05 * jax.random.normal(jax.random.fold_in(_tk, 500 + 15), (1250, 64), jnp.float32)
        tbl_16 = 0.05 * jax.random.normal(jax.random.fold_in(_tk, 500 + 16), (1000, 64), jnp.float32)
        tbl_17 = 0.05 * jax.random.normal(jax.random.fold_in(_tk, 500 + 17), (1250, 64), jnp.float32)
        tbl_18 = 0.05 * jax.random.normal(jax.random.fold_in(_tk, 500 + 18), (12500, 64), jnp.float32)
        tbl_19 = 0.05 * jax.random.normal(jax.random.fold_in(_tk, 500 + 19), (1000, 64), jnp.float32)
        tbl_20 = 0.05 * jax.random.normal(jax.random.fold_in(_tk, 500 + 20), (125000, 64), jnp.float32)
        tbl_21 = 0.05 * jax.random.normal(jax.random.fold_in(_tk, 500 + 21), (1250, 64), jnp.float32)
        tbl_22 = 0.05 * jax.random.normal(jax.random.fold_in(_tk, 500 + 22), (12500, 64), jnp.float32)
        tbl_23 = 0.05 * jax.random.normal(jax.random.fold_in(_tk, 500 + 23), (1000, 64), jnp.float32)
        tbl_24 = 0.05 * jax.random.normal(jax.random.fold_in(_tk, 500 + 24), (1250, 64), jnp.float32)
        tbl_25 = 0.05 * jax.random.normal(jax.random.fold_in(_tk, 500 + 25), (1000, 64), jnp.float32)
        _rk = jax.random.fold_in(_tk, 7)
        r_dense_t = 7.22013e-05 + 1.00017 * jax.random.normal(jax.random.fold_in(_rk, 101), (512, 256), jnp.float32)
        W_top1 = 0.0360844 * jax.random.normal(jax.random.fold_in(_tk, 801), (768, 512), jnp.float32)
        W_top2 = 0.0441942 * jax.random.normal(jax.random.fold_in(_tk, 802), (512, 256), jnp.float32)
        W_top3 = 0.0625 * jax.random.normal(jax.random.fold_in(_tk, 803), (256, 1), jnp.float32)
        b_top1 = jnp.zeros((512,), jnp.float32)
        b_top2 = jnp.zeros((256,), jnp.float32)
        return (r_dense_t, ids, tbl_0, tbl_1, tbl_2, tbl_3, tbl_4, tbl_5, tbl_6, tbl_7, tbl_8, tbl_9, tbl_10, tbl_11, tbl_12, tbl_13, tbl_14, tbl_15, tbl_16, tbl_17, tbl_18, tbl_19, tbl_20, tbl_21, tbl_22, tbl_23, tbl_24, tbl_25, W_top1, b_top1, W_top2, b_top2, W_top3)
    r_dense_t, ids, tbl_0, tbl_1, tbl_2, tbl_3, tbl_4, tbl_5, tbl_6, tbl_7, tbl_8, tbl_9, tbl_10, tbl_11, tbl_12, tbl_13, tbl_14, tbl_15, tbl_16, tbl_17, tbl_18, tbl_19, tbl_20, tbl_21, tbl_22, tbl_23, tbl_24, tbl_25, W_top1, b_top1, W_top2, b_top2, W_top3 = _rec_inputs()

    def _L0_rec_setup():
        import jax, jax.numpy as jnp
        import numpy as np
        EPS = 1e-05
        NI = 33
        TRIL_I, TRIL_J = np.tril_indices(NI, k=-1)

        def layer_norm(x, g, b):
            m = jnp.mean(x, axis=-1, keepdims=True)
            v = jnp.mean(jnp.square(x - m), axis=-1, keepdims=True)
            return (x - m) * jax.lax.rsqrt(v + EPS) * g + b
        key = jax.random.key(seed)
        ks = jax.random.split(key, 8)
        B, D_DENSE, N_SP, D_SP = (4096, 256, 26, 64)
        E, PROJ, MAXD, NFLAT = (128, 32, 512, 528)
        dense_t = jax.random.normal(ks[0], (B, D_DENSE), dtype=jnp.float32)
        sparse_t = jax.random.normal(ks[1], (B, N_SP, D_SP), dtype=jnp.float32)
        Wd = jax.random.normal(ks[2], (E, D_DENSE), dtype=jnp.float32) / np.sqrt(D_DENSE)
        Ws = jax.random.normal(ks[3], (E, D_SP), dtype=jnp.float32) / np.sqrt(D_SP)
        Wsi = jax.random.normal(ks[4], (PROJ, N_SP), dtype=jnp.float32) / np.sqrt(N_SP)
        Wl = jax.random.normal(ks[5], (MAXD, NFLAT), dtype=jnp.float32) / np.sqrt(NFLAT)
        gd = jnp.ones((E,), jnp.float32)
        bd = jnp.zeros((E,), jnp.float32)
        gs = jnp.ones((E,), jnp.float32)
        bs = jnp.zeros((E,), jnp.float32)
        gsi = jnp.ones((PROJ,), jnp.float32)
        bsi = jnp.zeros((PROJ,), jnp.float32)
        gl = jnp.ones((MAXD,), jnp.float32)
        bl = jnp.zeros((MAXD,), jnp.float32)
        return {'dense_t': dense_t, 'sparse_t': sparse_t, 'Wd': Wd, 'gd': gd, 'bd': bd, 'Ws': Ws, 'gs': gs, 'bs': bs, 'Wsi': Wsi, 'gsi': gsi, 'bsi': bsi, 'Wl': Wl, 'gl': gl, 'bl': bl, 'dims_in_use': 384}
    _L0_rec_all = _L0_rec_setup()
    _L0_rec_in = {k: v for k, v in _L0_rec_all.items() if k in ('Wd', 'gd', 'bd', 'Ws', 'gs', 'bs', 'Wsi', 'gsi', 'bsi', 'Wl', 'gl', 'bl')}
    del _L0_rec_all
    return {'r_dense_t': r_dense_t, 'ids': ids, 'tbl_0': tbl_0, 'tbl_1': tbl_1, 'tbl_2': tbl_2, 'tbl_3': tbl_3, 'tbl_4': tbl_4, 'tbl_5': tbl_5, 'tbl_6': tbl_6, 'tbl_7': tbl_7, 'tbl_8': tbl_8, 'tbl_9': tbl_9, 'tbl_10': tbl_10, 'tbl_11': tbl_11, 'tbl_12': tbl_12, 'tbl_13': tbl_13, 'tbl_14': tbl_14, 'tbl_15': tbl_15, 'tbl_16': tbl_16, 'tbl_17': tbl_17, 'tbl_18': tbl_18, 'tbl_19': tbl_19, 'tbl_20': tbl_20, 'tbl_21': tbl_21, 'tbl_22': tbl_22, 'tbl_23': tbl_23, 'tbl_24': tbl_24, 'tbl_25': tbl_25, 'W_top1': W_top1, 'b_top1': b_top1, 'W_top2': W_top2, 'b_top2': b_top2, 'W_top3': W_top3, 'L0_rec_Wd': _L0_rec_in['Wd'], 'L0_rec_gd': _L0_rec_in['gd'], 'L0_rec_bd': _L0_rec_in['bd'], 'L0_rec_Ws': _L0_rec_in['Ws'], 'L0_rec_gs': _L0_rec_in['gs'], 'L0_rec_bs': _L0_rec_in['bs'], 'L0_rec_Wsi': _L0_rec_in['Wsi'], 'L0_rec_gsi': _L0_rec_in['gsi'], 'L0_rec_bsi': _L0_rec_in['bsi'], 'L0_rec_Wl': _L0_rec_in['Wl'], 'L0_rec_gl': _L0_rec_in['gl'], 'L0_rec_bl': _L0_rec_in['bl']}

def reference(r_dense_t, ids, tbl_0, tbl_1, tbl_2, tbl_3, tbl_4, tbl_5, tbl_6, tbl_7, tbl_8, tbl_9, tbl_10, tbl_11, tbl_12, tbl_13, tbl_14, tbl_15, tbl_16, tbl_17, tbl_18, tbl_19, tbl_20, tbl_21, tbl_22, tbl_23, tbl_24, tbl_25, W_top1, b_top1, W_top2, b_top2, W_top3, L0_rec_Wd, L0_rec_gd, L0_rec_bd, L0_rec_Ws, L0_rec_gs, L0_rec_bs, L0_rec_Wsi, L0_rec_gsi, L0_rec_bsi, L0_rec_Wl, L0_rec_gl, L0_rec_bl):
    import jax
    import jax.numpy as jnp

    def _L0_rec_ref(dense_t, sparse_t, Wd, gd, bd, Ws, gs, bs, Wsi, gsi, bsi, Wl, gl, bl, dims_in_use):
        import jax, jax.numpy as jnp
        import numpy as np
        EPS = 1e-05
        NI = 33
        TRIL_I, TRIL_J = np.tril_indices(NI, k=-1)

        def layer_norm(x, g, b):
            m = jnp.mean(x, axis=-1, keepdims=True)
            v = jnp.mean(jnp.square(x - m), axis=-1, keepdims=True)
            return (x - m) * jax.lax.rsqrt(v + EPS) * g + b
        x = layer_norm(dense_t @ Wd.T, gd, bd)
        y = layer_norm(jnp.einsum('bnd,ed->bne', sparse_t, Ws), gs, bs)
        y = jnp.einsum('bne,pn->bep', y, Wsi)
        y = layer_norm(y, gsi, bsi)
        y = jnp.swapaxes(y, 1, 2)
        T = jnp.concatenate([x[:, None, :], y], axis=1)
        Z = jnp.einsum('bnd,bmd->bnm', T, T)
        Zflat = Z[:, TRIL_I, TRIL_J]
        out = layer_norm(Zflat @ Wl.T, gl, bl)
        maxd = out.shape[-1]
        mask = (jnp.arange(maxd) < dims_in_use).astype(out.dtype)
        return out * mask
    e = jnp.stack([tbl_0[ids[:, 0]], tbl_1[ids[:, 1]], tbl_2[ids[:, 2]], tbl_3[ids[:, 3]], tbl_4[ids[:, 4]], tbl_5[ids[:, 5]], tbl_6[ids[:, 6]], tbl_7[ids[:, 7]], tbl_8[ids[:, 8]], tbl_9[ids[:, 9]], tbl_10[ids[:, 10]], tbl_11[ids[:, 11]], tbl_12[ids[:, 12]], tbl_13[ids[:, 13]], tbl_14[ids[:, 14]], tbl_15[ids[:, 15]], tbl_16[ids[:, 16]], tbl_17[ids[:, 17]], tbl_18[ids[:, 18]], tbl_19[ids[:, 19]], tbl_20[ids[:, 20]], tbl_21[ids[:, 21]], tbl_22[ids[:, 22]], tbl_23[ids[:, 23]], tbl_24[ids[:, 24]], tbl_25[ids[:, 25]]], axis=1)
    z = _L0_rec_ref(r_dense_t, e, L0_rec_Wd, L0_rec_gd, L0_rec_bd, L0_rec_Ws, L0_rec_gs, L0_rec_bs, L0_rec_Wsi, L0_rec_gsi, L0_rec_bsi, L0_rec_Wl, L0_rec_gl, L0_rec_bl, 384)
    z = z.reshape(z.shape[0], -1)
    h = jnp.concatenate([z, r_dense_t], axis=1)
    h = jnp.maximum(h @ W_top1 + b_top1, 0.0)
    h = jnp.maximum(h @ W_top2 + b_top2, 0.0)
    y = h @ W_top3
    return y

_drawn_inputs = setup_inputs


def setup_inputs(seed=0):
    import zlib

    import numpy as np

    out = dict(_drawn_inputs(seed))
    spreads = {'b_top1': (0.0, 0.1),
     'b_top2': (0.0, 0.1),
     'L0_rec_gd': (1.0, 0.6),
     'L0_rec_bd': (0.0, 0.8),
     'L0_rec_gs': (1.0, 0.6),
     'L0_rec_bs': (0.0, 0.1),
     'L0_rec_gsi': (1.0, 0.2),
     'L0_rec_bsi': (0.0, 0.1),
     'L0_rec_gl': (1.0, 0.2),
     'L0_rec_bl': (0.0, 0.1)}
    factors = {}
    for name, (base, spread) in spreads.items():
        noise = np.random.default_rng([zlib.crc32(name.encode()), seed]).standard_normal(out[name].shape)
        drawn = base * np.exp(spread * noise) if base else spread * noise
        out[name] = jnp.asarray(drawn.astype(out[name].dtype))
    for name, factor in factors.items():
        out[name] = (out[name] * factor).astype(out[name].dtype)
    return out
```

```python
from contextlib import ExitStack

import concourse.bass as bass
from concourse import mybir

F32 = mybir.dt.float32
F16 = mybir.dt.float16
I32 = mybir.dt.int32
ALU = mybir.AluOpType
ACT = mybir.ActivationFunctionType
AX_X = mybir.AxisListType.X

P = 128
B = 512
NF = 26
D = 64
E = 128
NPROJ = 32
DENSE = 256
L = 512
LIVE = 384
H1, H2 = 512, 256
EPS = 1e-5

GROUP = 64
GRAN = 2 * GROUP
NG = B // GRAN
TILES = GROUP * NF // P
BATCH_END = [4, 7, 10, 13]
NC = len(BATCH_END)
CB = GROUP // NC
CHUNK = 2 * CB
SPAN = 6
SLOTS = NPROJ + 2
X_SLOT, ONE_SLOT = NPROJ, NPROJ + 1
ZCOLS = NPROJ + 1
KB = 8
LC, LLIVE = L // P, LIVE // P
OC1, OC2 = H1 // P, H2 // P
ROW_ONE, ROW_X, ROW_S = 0, 32, 96
(C_GD, C_BD, C_GL, C_BL, C_B1, C_B2, C_W3, C_GI, C_BI, C_GJ, C_BJ, C_XM, C_END) = (
    0, 1, 2, 5, 8, 12, 14, 16, 17, 18, 26, 34, 42)


def batch(c):
    return range(BATCH_END[c - 1] if c else 0, BATCH_END[c])


def tile_spans(j):
    b0, b1 = P * j // NF, (P * j + P - 1) // NF + 1
    out = []
    while b0 < b1:
        end = min(b1, (b0 // CB + 1) * CB)
        out.append((b0 // CB, (b0 % CB) * NPROJ, (b0 - P * j // NF) * NPROJ, (end - b0) * NPROJ))
        b0 = end
    return out


def dlrm_tower(nc, ids, base, table, ws_t, gs_row, ident, small, pair_mask, wsi_blocks, block_mask, wsi_small,
               bs_rep, wd_t, dense_t, wl_blocks, w1_z, w1_d, w2, out):
    with ExitStack() as ctx:
        def sb(name, shape, dt=F32):
            return ctx.enter_context(nc.sbuf_tensor(name, shape, dt))

        def sem(name):
            return ctx.enter_context(nc.semaphore(name))

        idx_in = sb("idx_in", [P, NG * 2 * TILES], I32)
        idx_base = sb("idx_base", [P, NG * 2 * TILES], I32)
        idx = sb("idx", [P, NG * 2 * TILES], I32)
        wc = sb("wc", [P, E])
        wc_nat = sb("wc_nat", [P, P])
        gram = sb("gram", [P, P])
        wcg = sb("wcg", [P, E])
        gs_sb = sb("gs_sb", [P, E])
        eye = sb("eye", [P, P])
        ones = sb("ones", [P, P])
        sm = sb("sm", [P, C_END])
        pmask = sb("pmask", [P, KB * 33 + 32])
        S = sb("S", [P, TILES, SPAN * NPROJ])
        smask = sb("smask", [P, TILES, SPAN * NPROJ], F16)
        smean = sb("smean", [P, TILES])
        wsis = sb("wsis", [NF, NPROJ])
        bsr = sb("bsr", [NF, E])
        tiny = sb("tiny", [P, 16])
        bias_y = sb("bias_y", [P, NPROJ])
        wd = sb("wd", [P, 2, E])
        dns = sb("dns", [P, 2, B])
        wl = sb("wl", [P, KB + 1, L])
        kcoef = sb("kcoef", [P, 4 * KB])
        dmat = sb("dmat", [P, KB, P])
        w1z = sb("w1z", [P, LLIVE, H1])
        w1d = sb("w1d", [P, 2, H1])
        w2s = sb("w2s", [P, OC1, H2])
        b1e = sb("b1e", [P, OC1])
        eps = sb("eps", [P, 1])
        x_sb = sb("x_sb", [P, B])
        x_sq = sb("x_sq", [P, B])
        x_r = sb("x_r", [P, B])
        h1_dense = sb("h1_dense", [P, OC1, B])
        G = sb("G", [P, TILES, 2, D])
        gt = sb("gt", [P, 4 * P])
        qg = sb("qg", [P, 4 * P])
        var1 = sb("var1", [P, 8])
        sd1 = sb("sd1", [P, 8])
        r1 = sb("r1", [P, 8])
        ut = sb("ut", [P, 512])
        V = sb("V", [P, GRAN, SLOTS])
        sq2 = sb("sq2", [P, CHUNK, NPROJ])
        var2 = sb("var2", [P, CHUNK])
        sd2 = sb("sd2", [P, CHUNK])
        r2 = sb("r2", [P, CHUNK])
        zb = sb("zb", [P, KB, GRAN])
        z8 = sb("z8", [P, B])
        f_sb = sb("f_sb", [P, LC, GRAN])
        f_sq = sb("f_sq", [P, LC, GRAN])
        sd3 = sb("sd3", [P, GRAN])
        r3 = sb("r3", [P, GRAN])
        zn = sb("zn", [P, LLIVE, GRAN])
        h1_pre = sb("h1_pre", [P, OC1, GRAN])
        h1 = sb("h1", [P, OC1, GRAN])
        h2 = sb("h2", [P, OC2, GRAN])
        y_row = sb("y_row", [1, B])
        ps_gq = ctx.enter_context(nc.psum_tensor("ps_gq", [P, 512], F32))
        ps_tail = ctx.enter_context(nc.psum_tensor("ps_tail", [P, 512], F32))
        ps_ut = ctx.enter_context(nc.psum_tensor("ps_ut", [P, 2, 512], F32))
        ps_y = ctx.enter_context(nc.psum_tensor("ps_y", [P, 2, 512], F32))
        ps_z = ctx.enter_context(nc.psum_tensor("ps_z", [P, 2, 512], F32))

        ld_ids, ld_ws, ld_sm, ld_s, ld_x, ld_wl, ld_w1, ld_w2 = [
            sem(n) for n in ("ld_ids", "ld_ws", "ld_sm", "ld_s", "ld_x", "ld_wl", "ld_w1", "ld_w2")]
        idx_ready = sem("idx_ready")
        gathered = [sem(f"gathered{c}") for c in range(NC)]
        set_dve, set_pe, set_act = sem("set_dve"), sem("set_pe"), sem("set_act")
        gt_ps, gt_sb, q_ps, q_used = sem("gt_ps"), sem("gt_sb"), sem("q_ps"), sem("q_used")
        var1_ready, sd1_ready, r1_ready, g_scaled = sem("var1_ready"), sem("sd1_ready"), sem("r1_ready"), sem("g_scaled")
        ut_ps, ut_sb, y_ps, y_sb = sem("ut_ps"), sem("ut_sb"), sem("y_ps"), sem("y_sb")
        sq_ready, var2_ready, sd2_ready, r2_ready, v_ready = (
            sem("sq_ready"), sem("var2_ready"), sem("sd2_ready"), sem("r2_ready"), sem("v_ready"))
        z_ps, z_sb, f_ps, f_ready, ss_ps = sem("z_ps"), sem("z_sb"), sem("f_ps"), sem("f_ready"), sem("ss_ps")
        sd3_ready, r3_ready, zn_ready = sem("sd3_ready"), sem("r3_ready"), sem("zn_ready")
        h1_ps, h1_pre_ready, h1_ready, h2_ps, h2_ready = (
            sem("h1_ps"), sem("h1_pre_ready"), sem("h1_ready"), sem("h2_ps"), sem("h2_ready"))
        yo_ps, yo_ready, stored = sem("yo_ps"), sem("yo_ready"), sem("stored")

        v_flat = V[:, :, :]

        def chunk_v(c, lo=0, hi=NPROJ):
            return V[:, c * CHUNK:(c + 1) * CHUNK, lo:hi]

        def upto(gp, per, k):
            return gp * per + k

        block = ctx.enter_context(nc.Block())

        @block.sync
        def _(sp):
            sp.dma_start(idx_in[:, :], ids).then_inc(ld_ids, 16)
            sp.dma_start(idx_base[:, :], base).then_inc(ld_ids, 16)
            sp.dma_start(wc[:, :], ws_t).then_inc(ld_ws, 16)
            sp.dma_start(eye[:, :], ident).then_inc(ld_ws, 16)
            sp.dma_start(gs_sb[:, :], gs_row).then_inc(ld_ws, 16)
            sp.dma_start(sm[:, :], small).then_inc(ld_sm, 16)
            sp.dma_start(pmask[:, :], pair_mask).then_inc(ld_sm, 16)
            sp.dma_start(S[:, :, :], wsi_blocks).then_inc(ld_s, 16)
            sp.dma_start(smask[:, :, :], block_mask).then_inc(ld_s, 16)
            sp.dma_start(wsis[:, :], wsi_small).then_inc(ld_s, 16)
            sp.dma_start(bsr[:, :], bs_rep).then_inc(ld_s, 16)
            sp.dma_start(w2s[:, :, :], w2).then_inc(ld_w2, 16)
            sp.wait_ge(yo_ready, NG)
            sp.dma_start(out.rearrange("b o -> o b"), y_row[:, :]).then_inc(stored, 16)
            sp.wait_ge(stored, 16)

        @block.gpsimd
        def _(pool):
            pool.wait_ge(idx_ready, 1)

            for gp in range(NG):
                for c in range(NC):
                    if gp:
                        pool.wait_ge(ut_ps, upto(gp - 1, NC, c + 1))
                    for j in batch(c):
                        for g in range(2):
                            k = gp * 2 * TILES + 2 * j + g
                            pool.indirect_dma_start(
                                G[:, j, g, :], None, table,
                                bass.IndirectOffsetOnAxis(ap=idx[:, k:k + 1], axis=0)).then_inc(gathered[c], 16)

        @block.scalar
        def _(act):
            act.dma_start(wd[:, :, :], wd_t).then_inc(ld_x, 16)
            act.dma_start(dns[:, :, :], dense_t).then_inc(ld_x, 16)
            act.dma_start(w1z[:, :, :], w1_z).then_inc(ld_w1, 16)
            act.dma_start(w1d[:, :, :], w1_d).then_inc(ld_w1, 16)
            act.dma_start(wl[:, 0:KB, :], wl_blocks).then_inc(ld_wl, 16)
            act.wait_ge(set_pe, 1)
            act.copy(wc_nat[:, :], ps_ut[:, 0, 0:P]).then_inc(set_act, 1)
            act.wait_ge(set_pe, 3)
            act.copy(bias_y[:, :], ps_y[:, 0, 0:NPROJ]).then_inc(set_act, 1)
            act.wait_ge(set_pe, 4)
            act.activation(x_sq[:, :], ps_y[:, 1, :], ACT.Square).then_inc(set_act, 1)
            act.wait_ge(set_pe, 5)
            act.wait_ge(set_dve, 1)
            act.activation(x_r[:, :], ps_z[:, 0, :], ACT.Sqrt, bias=eps[:, :], scale=1.0 / E).then_inc(set_act, 1)
            act.wait_ge(set_dve, 4)
            for oc in range(OC1):
                act.wait_ge(set_pe, 7 + oc)
                act.activation(h1_dense[:, oc, :], ps_ut[:, oc % 2, :], ACT.Identity,
                               bias=b1e[:, oc:oc + 1]).then_inc(set_act, 1)
            act.wait_ge(set_pe, 11)
            act.wait_ge(set_dve, 1)
            act.copy(z8[ROW_X:ROW_X + 1, :], ps_z[ROW_X:ROW_X + 1, 0, :]).then_inc(set_act, 1)
            act.wait_ge(set_pe, 12)
            act.copy(wl[:, KB, :], ps_z[:, 1, :]).then_inc(set_act, 1)

            def gt_copy(gp, c):
                n = len(batch(c)) * P
                act.wait_ge(gt_ps, upto(gp, NC, c + 1))
                act.copy(gt[:, 0:n], ps_gq[:, 0:n]).then_inc(gt_sb, 1)

            def deviation1(gp, c):
                n = len(batch(c)) * 2
                act.wait_ge(var1_ready, upto(gp, NC, c + 1))
                act.activation(sd1[:, 0:n], var1[:, 0:n], ACT.Sqrt, bias=eps[:, :], scale=1.0 / E).then_inc(sd1_ready, 1)

            def ut_copy(gp, c):
                act.wait_ge(ut_ps, upto(gp, NC, c + 1))
                act.copy(ut[:, :], ps_ut[:, c % 2, :]).then_inc(ut_sb, 1)

            def square2(gp, c):
                act.wait_ge(y_sb, upto(gp, 2 * NC, 2 * c + 2))
                act.activation(sq2[:, :, :], chunk_v(c), ACT.Square).then_inc(sq_ready, 1)

            def deviation2(gp, c):
                act.wait_ge(var2_ready, upto(gp, NC, c + 1))
                act.activation(sd2[:, :], var2[:, :], ACT.Sqrt, bias=eps[:, :], scale=1.0 / NPROJ).then_inc(sd2_ready, 1)

            def z_copy(gp, h):
                act.wait_ge(z_ps, upto(gp, 2, h + 1))
                for qb in range(4):
                    src = ps_z[32 * qb:32 * qb + 32, :, 0:8 * ZCOLS].rearrange("p w (b c) -> p w b c", c=ZCOLS)
                    b0 = h * 64 + 16 * qb
                    for q in range(4):
                        dst = zb[32 * q:32 * q + 32, :, b0:b0 + 16].rearrange("p k (w b) -> p w b k", w=2)
                        act.copy(dst, src[:, :, :, 8 * q:8 * q + 8])
                    last = act.copy(z8[ROW_S:ROW_S + 32, bass.ds(gp * GRAN + b0, 16)].rearrange("p (w b) -> p w b", w=2),
                                    src[:, :, :, ZCOLS - 1])
                last.then_inc(z_sb, 1)

            def f_copy(gp):
                act.wait_ge(f_ps, upto(gp, 1, 1))
                act.copy(f_sb[:, :, :].rearrange("p c b -> p (c b)"), ps_tail[:, :])
                act.activation(f_sq[:, :, :].rearrange("p c b -> p (c b)"), ps_tail[:, :], ACT.Square).then_inc(f_ready, 1)

            def deviation3(gp):
                act.wait_ge(ss_ps, upto(gp, 1, 1))
                act.activation(sd3[:, :], ps_tail[:, 0:GRAN], ACT.Sqrt, bias=eps[:, :], scale=1.0 / L).then_inc(sd3_ready, 1)

            def relu1(gp):
                act.wait_ge(h1_pre_ready, upto(gp, 1, 1))
                act.activation(h1[:, :, :], h1_pre[:, :, :], ACT.Relu).then_inc(h1_ready, 1)

            def relu2(gp):
                act.wait_ge(h2_ps, upto(gp, 1, 1))
                for oc in range(OC2):
                    last = act.activation(h2[:, oc, :], ps_tail[:, oc * GRAN:(oc + 1) * GRAN], ACT.Relu,
                                          bias=sm[:, C_B2 + oc:C_B2 + oc + 1])
                last.then_inc(h2_ready, 1)

            def y_copy(gp):
                act.wait_ge(yo_ps, upto(gp, 1, 1))
                act.copy(y_row[:, bass.ds(gp * GRAN, GRAN)], ps_tail[0:1, 0:GRAN]).then_inc(yo_ready, 1)

            def body(gp, back):
                gt_copy(gp, 0)
                deviation1(gp, 0)
                gt_copy(gp, 1)
                ut_copy(gp, 0)
                if back:
                    z_copy(gp - 1, 1)
                square2(gp, 0)
                deviation2(gp, 0)
                deviation1(gp, 1)
                ut_copy(gp, 1)
                square2(gp, 1)
                deviation2(gp, 1)
                gt_copy(gp, 2)
                deviation1(gp, 2)
                ut_copy(gp, 2)
                square2(gp, 2)
                deviation2(gp, 2)
                gt_copy(gp, 3)
                if back:
                    f_copy(gp - 1)
                deviation1(gp, 3)
                if back:
                    deviation3(gp - 1)
                ut_copy(gp, 3)
                z_copy(gp, 0)
                if back:
                    relu1(gp - 1)
                square2(gp, 3)
                deviation2(gp, 3)
                if back:
                    relu2(gp - 1)
                    y_copy(gp - 1)

            body(0, False)
            with act.Fori(1, NG) as gp:
                body(gp, True)
            z_copy(NG - 1, 1)
            f_copy(NG - 1)
            deviation3(NG - 1)
            relu1(NG - 1)
            relu2(NG - 1)
            y_copy(NG - 1)

        @block.vector
        def _(dve):
            chain = sem("dve_chain")
            count = [0]

            def link(ins):
                count[0] += 1
                ins.then_inc(chain, 1)
                dve.wait_ge(chain, count[0])

            dve.wait_ge(ld_ids, 32)
            dve.tensor_tensor(idx[:, :], idx_in[:, :], idx_base[:, :], ALU.add).then_inc(idx_ready, 1)
            dve.memset(eps[:, :], EPS)
            dve.memset(ones[:, :], 1.0)
            dve.memset(gram[:, :], 0.0)
            link(dve.memset(z8[:, :], 0.0))
            dve.memset(z8[ROW_ONE:ROW_ONE + 1, :], 1.0)
            dve.memset(dmat[:, :, :], 0.0)
            link(dve.memset(V[:, :, ONE_SLOT], 1.0))
            dve.sem_inc(set_dve, 1)
            dve.wait_ge(ld_ws, 48)
            link(dve.reduce_sum(tiny[:, 0:1], wc[:, :], AX_X))
            link(dve.tensor_scalar(tiny[:, 0:1], tiny[:, 0:1], -1.0 / E, None, ALU.mult))
            link(dve.tensor_scalar(wc[:, :], wc[:, :], tiny[:, 0:1], None, ALU.add))
            dve.tensor_tensor(wcg[:, :], wc[:, :], gs_sb[:, :], ALU.mult).then_inc(set_dve, 1)
            dve.wait_ge(ld_s, 64)
            link(dve.reduce_sum(tiny[0:NF, 1:2], wsis[:, :], AX_X))
            link(dve.tensor_scalar(tiny[0:NF, 1:2], tiny[0:NF, 1:2], -1.0 / NPROJ, None, ALU.mult))
            link(dve.tensor_scalar(wsis[:, :], wsis[:, :], tiny[0:NF, 1:2], None, ALU.add))
            dve.wait_ge(ld_x, 32)
            link(dve.reduce_sum(tiny[:, 2:4], wd[:, :, :], AX_X))
            link(dve.tensor_scalar(tiny[:, 2:4], tiny[:, 2:4], -1.0 / E, None, ALU.mult))
            for k in range(2):
                last = dve.tensor_scalar(wd[:, k, :], wd[:, k, :], tiny[:, 2 + k:3 + k], None, ALU.add)
            last.then_inc(set_dve, 1)
            dve.wait_ge(set_pe, 2)
            for h in (0, 64):
                last = dve.tensor_copy(gram[h:h + 64, h:h + 64], ps_ut[h:h + 64, 1, h:h + 64])
            link(last)
            dve.wait_ge(ld_sm, 32)
            dve.wait_ge(set_pe, 6)
            link(dve.tensor_tensor(b1e[:, :], ps_gq[:, 0:OC1], sm[:, C_B1:C_B1 + OC1], ALU.add))
            dve.sem_inc(set_dve, 1)
            link(dve.reduce_sum(smean[:, :], S[:, :, :], AX_X))
            link(dve.tensor_scalar(smean[:, :], smean[:, :], -1.0 / NPROJ, None, ALU.mult))
            for j in range(TILES):
                last = dve.scalar_tensor_tensor(S[:, j, :], smask[:, j, :], smean[:, j:j + 1], S[:, j, :],
                                                ALU.mult, ALU.add)
            last.then_inc(set_dve, 1)
            dve.wait_ge(set_act, 4)
            link(dve.reciprocal(x_sq[:, :], x_r[:, :]))
            link(dve.tensor_tensor(x_sb[:, :], ps_y[:, 1, :], x_sq[:, :], ALU.mult))
            link(dve.tensor_scalar(x_sb[:, :], x_sb[:, :], sm[:, C_GD:C_GD + 1], sm[:, C_BD:C_BD + 1],
                                   ALU.mult, ALU.add))
            dve.sem_inc(set_dve, 1)
            for k in range(LLIVE):
                dve.tensor_scalar(w1z[:, k, :], w1z[:, k, :], sm[:, C_GL + k:C_GL + k + 1], None, ALU.mult)
            dve.wait_ge(ld_wl, 16)
            link(dve.reduce_sum(tiny[:, 4:4 + KB], wl[:, 0:KB, :], AX_X))
            link(dve.tensor_scalar(tiny[:, 4:4 + KB], tiny[:, 4:4 + KB], -1.0 / L, None, ALU.mult))
            for k in range(KB):
                dve.tensor_scalar(wl[:, k, :], wl[:, k, :], tiny[:, 4 + k:5 + k], None, ALU.add)
            gj, bj, xm = (sm[:, c:c + KB] for c in (C_GJ, C_BJ, C_XM))
            gi, bi = sm[:, C_GI:C_GI + 1], sm[:, C_BI:C_BI + 1]
            k_gb, k_bg, k_bb, k_gg = (kcoef[:, n * KB:(n + 1) * KB] for n in range(4))
            dve.tensor_scalar(k_gb, bj, gi, None, ALU.mult)
            dve.tensor_scalar(k_bg, gj, bi, None, ALU.mult)
            dve.tensor_scalar(k_bb, bj, bi, float(E), ALU.mult, ALU.mult)
            link(dve.tensor_scalar(k_gg, gj, gi, None, ALU.mult))
            pm = pmask[:, 0:KB * 33].rearrange("p (k c) -> p k c", c=33)
            delta = pmask[:, KB * 33:KB * 33 + 32]
            bg_wide = k_bg.unsqueeze(2)
            dve.tensor_tensor(dmat[:, :, ROW_X], pm[:, :, 32], k_bg, ALU.mult)
            dve.tensor_copy(dmat[:, :, ROW_ONE], k_bb)
            link(dve.tensor_tensor(dmat[:, :, ROW_S:ROW_S + 32], pm[:, :, 0:32], bg_wide.broadcast_to([P, KB, 32]), ALU.mult))
            for k in range(KB):
                last = dve.scalar_tensor_tensor(dmat[:, k, ROW_S:ROW_S + 32], delta, k_gb[:, k:k + 1],
                                                dmat[:, k, ROW_S:ROW_S + 32], ALU.mult, ALU.add)
            last.then_inc(set_dve, 1)
            dve.wait_ge(set_pe, 12)
            for k in range(KB):
                last = dve.tensor_scalar(wl[:, k, :], wl[:, k, :], k_gg[:, k:k + 1], None, ALU.mult)
            last.then_inc(set_dve, 1)

            def variance1(gp, c):
                js = batch(c)
                n = len(js)
                dve.wait_ge(q_ps, upto(gp, NC, c + 1))
                dve.tensor_tensor(qg[:, 0:n * P], ps_gq[:, 0:n * P],
                                  G[:, js[0]:js[0] + n, :, :].rearrange("p j g d -> p (j g d)"),
                                  ALU.mult).then_inc(q_used, 1)
                dve.wait_ge(q_used, upto(gp, NC, c + 1))
                dve.reduce_sum(var1[:, 0:2 * n], qg[:, 0:n * P].rearrange("p (t d) -> p t d", d=D), AX_X).then_inc(var1_ready, 1)

            def scale_rows(gp, c):
                js = batch(c)
                n = 2 * len(js)
                dve.wait_ge(sd1_ready, upto(gp, NC, c + 1))
                dve.reciprocal(r1[:, 0:n], sd1[:, 0:n]).then_inc(r1_ready, 1)
                dve.wait_ge(r1_ready, upto(gp, NC, c + 1))
                rows = G[:, js[0]:js[0] + n // 2, :, :].rearrange("p j g d -> p (j g) d")
                dve.tensor_tensor(rows, rows, r1[:, 0:n].unsqueeze(2).broadcast_to([P, n, D]), ALU.mult).then_inc(g_scaled, 1)

            def y_evacuate(gp, c, back):
                if back:
                    dve.wait_ge(z_ps, upto(gp - 1, 2, c // 2 + 1))
                if c % 2 == 0:
                    dve.tensor_copy(V[:, c * CHUNK:c * CHUNK + 2 * CHUNK, X_SLOT],
                                    x_sb[:, bass.ds(gp * GRAN + c * CHUNK, 2 * CHUNK)])
                for g in range(2):
                    dve.wait_ge(y_ps, upto(gp, 2 * NC, 2 * c + g + 1))
                    b0 = c * CHUNK + g * CB
                    dve.tensor_tensor(V[:, b0:b0 + CB, 0:NPROJ], ps_y[:, g, :].rearrange("p (b q) -> p b q", q=NPROJ),
                                      bias_y[:, :].unsqueeze(1).broadcast_to([P, CB, NPROJ]), ALU.add).then_inc(y_sb, 1)

            def normalise2(gp, c):
                dve.wait_ge(sq_ready, upto(gp, NC, c + 1))
                dve.reduce_sum(var2[:, :], sq2[:, :, :], AX_X).then_inc(var2_ready, 1)
                dve.wait_ge(sd2_ready, upto(gp, NC, c + 1))
                dve.reciprocal(r2[:, :], sd2[:, :]).then_inc(r2_ready, 1)
                dve.wait_ge(r2_ready, upto(gp, NC, c + 1))
                dve.tensor_tensor(chunk_v(c), chunk_v(c), r2[:, :].unsqueeze(2).broadcast_to([P, CHUNK, NPROJ]),
                                  ALU.mult).then_inc(v_ready, 1)

            def normalise3(gp):
                dve.wait_ge(sd3_ready, upto(gp, 1, 1))
                dve.reciprocal(r3[:, :], sd3[:, :]).then_inc(r3_ready, 1)
                dve.wait_ge(r3_ready, upto(gp, 1, 1))
                dve.tensor_tensor(zn[:, :, :], f_sb[:, 0:LLIVE, :], r3[:, :].unsqueeze(1).broadcast_to([P, LLIVE, GRAN]),
                                  ALU.mult).then_inc(zn_ready, 1)

            def add_dense(gp):
                dve.wait_ge(h1_ps, upto(gp, 1, 1))
                dve.tensor_tensor(h1_pre[:, :, :], ps_tail[:, :].rearrange("p (c b) -> p c b", b=GRAN),
                                  h1_dense[:, :, bass.ds(gp * GRAN, GRAN)], ALU.add).then_inc(h1_pre_ready, 1)

            def body(gp, back):
                for c in range(NC):
                    variance1(gp, c)
                    scale_rows(gp, c)
                    if back and c == 3:
                        normalise3(gp - 1)
                        add_dense(gp - 1)
                    y_evacuate(gp, c, back)
                    normalise2(gp, c)

            body(0, False)
            with dve.Fori(1, NG) as gp:
                body(gp, True)
            normalise3(NG - 1)
            add_dense(NG - 1)

        @block.tensor
        def _(pe):
            pe.wait_ge(ld_ws, 48)
            pe.wait_ge(set_dve, 2)
            pe.transpose(ps_ut[:, 0, 0:P], wc[:, :], eye[:, :]).then_inc(set_pe, 1)
            pe.wait_ge(set_act, 1)
            pe.matmul(ps_ut[:, 1, 0:P], wc_nat[:, :], wc_nat[:, :], start=True, stop=True).then_inc(set_pe, 1)
            pe.wait_ge(set_dve, 3)
            pe.wait_ge(ld_s, 64)
            pe.matmul(ps_y[:, 0, 0:NPROJ], bsr[:, :], wsis[:, :], start=True, stop=True).then_inc(set_pe, 1)
            for k in range(2):
                mm = pe.matmul(ps_y[:, 1, :], wd[:, k, :], dns[:, k, :], start=(k == 0), stop=(k == 1))
            mm.then_inc(set_pe, 1)
            pe.wait_ge(set_act, 3)
            pe.matmul(ps_z[:, 0, :], ones[:, :], x_sq[:, :], start=True, stop=True).then_inc(set_pe, 1)
            pe.wait_ge(ld_w1, 32)
            pe.wait_ge(ld_sm, 32)
            for oc in range(OC1):
                for k in range(LLIVE):
                    mm = pe.matmul(ps_gq[:, oc:oc + 1], w1z[:, k, oc * P:(oc + 1) * P], sm[:, C_BL + k:C_BL + k + 1],
                                   start=(k == 0), stop=(k == LLIVE - 1))
            mm.then_inc(set_pe, 1)
            pe.wait_ge(set_act, 1)
            pe.wait_ge(set_dve, 4)
            for oc in range(OC1):
                if oc >= 2:
                    pe.wait_ge(set_act, 3 + oc)
                for k in range(2):
                    mm = pe.matmul(ps_ut[:, oc % 2, :], w1d[:, k, oc * P:(oc + 1) * P], dns[:, k, :],
                                   start=(k == 0), stop=(k == 1))
                mm.then_inc(set_pe, 1)
            pe.wait_ge(set_act, 4)
            pe.wait_ge(set_dve, 6)
            pe.matmul(ps_z[ROW_X:ROW_X + 1, 0, :], ones[:, 0:1], x_sb[:, :], start=True, stop=True).then_inc(set_pe, 1)
            pe.wait_ge(set_dve, 7)
            for k in range(KB):
                mm = pe.matmul(ps_z[:, 1, :], dmat[:, k, :], wl[:, k, :], start=(k == 0), stop=(k == KB - 1))
            mm.then_inc(set_pe, 1)

            def transpose_rows(gp, c, back):
                js = batch(c)
                pe.wait_ge(gathered[c], upto(gp, 2 * len(js) * 16, 2 * len(js) * 16))
                if back or c:
                    pe.wait_ge(q_used, upto(gp, NC, c))
                for n, j in enumerate(js):
                    mm = pe.transpose(ps_gq[:, n * P:(n + 1) * P], G[:, j, :, :].rearrange("p g d -> p (g d)"), eye[:, :])
                mm.then_inc(gt_ps, 1)

            def gram_rows(gp, c):
                pe.wait_ge(gt_sb, upto(gp, NC, c + 1))
                for n in range(len(batch(c))):
                    mm = pe.matmul(ps_gq[:, n * P:(n + 1) * P], gt[:, n * P:(n + 1) * P], gram[:, :], start=True, stop=True)
                mm.then_inc(q_ps, 1)

            def project_fields(gp, c, back):
                pe.wait_ge(g_scaled, upto(gp, NC, c + 1))
                if back or c:
                    pe.wait_ge(ut_sb, upto(gp, NC, c))
                for j in batch(c):
                    for chunk, col, scol, n in tile_spans(j):
                        first = j == 0 or (P * j // NF) // CB != chunk or (P * j) % (CB * NF) == 0
                        mm = pe.matmul(ps_ut[:, chunk % 2, col:col + n], G[:, j, :, :].rearrange("p g d -> p (g d)"),
                                       S[:, j, scol:scol + n], start=first, stop=True, skip_group_check=True)
                mm.then_inc(ut_ps, 1)

            def embed(gp, c, back):
                pe.wait_ge(ut_sb, upto(gp, NC, c + 1))
                for g in range(2):
                    if back or c:
                        pe.wait_ge(y_sb, upto(gp, 2 * NC, 2 * c + g - 1))
                    pe.matmul(ps_y[:, g, :], wcg[64 * g:64 * g + 64, :], ut[64 * g:64 * g + 64, :],
                              start=True, stop=True).then_inc(y_ps, 1)

            def pair_products(gp, h, back):
                pe.wait_ge(v_ready, upto(gp, NC, 2 * h + 2))
                if back or h:
                    pe.wait_ge(z_sb, upto(gp, 2, h))
                for bb in range(16):
                    for qb in range(4):
                        b = h * 64 + 16 * qb + bb
                        col = (bb % 8) * ZCOLS
                        mm = pe.matmul(ps_z[32 * qb:32 * qb + 32, bb // 8, col:col + ZCOLS], V[:, b, 0:NPROJ],
                                       V[:, b, 1:SLOTS], start=True, stop=True)
                mm.then_inc(z_ps, 1)

            def project_pairs(gp, lc, back):
                if lc == 0:
                    pe.wait_ge(z_sb, upto(gp, 2, 2))
                    if back:
                        pe.wait_ge(yo_ready, gp)
                for k in range(KB + 1):
                    rhs = zb[:, k, :] if k < KB else z8[:, bass.ds(gp * GRAN, GRAN)]
                    mm = pe.matmul(ps_tail[:, lc * GRAN:(lc + 1) * GRAN], wl[:, k, lc * P:(lc + 1) * P], rhs,
                                   start=(k == 0), stop=(k == KB))
                if lc == LC - 1:
                    mm.then_inc(f_ps, 1)

            def sum_squares(gp):
                pe.wait_ge(f_ready, upto(gp, 1, 1))
                for lc in range(LC):
                    mm = pe.matmul(ps_tail[:, 0:GRAN], ones[:, :], f_sq[:, lc, :], start=(lc == 0), stop=(lc == LC - 1))
                mm.then_inc(ss_ps, 1)

            def layer1(gp):
                pe.wait_ge(zn_ready, upto(gp, 1, 1))
                for oc in range(OC1):
                    for k in range(LLIVE):
                        mm = pe.matmul(ps_tail[:, oc * GRAN:(oc + 1) * GRAN], w1z[:, k, oc * P:(oc + 1) * P], zn[:, k, :],
                                       start=(k == 0), stop=(k == LLIVE - 1))
                mm.then_inc(h1_ps, 1)

            def layer2(gp):
                pe.wait_ge(h1_ready, upto(gp, 1, 1))
                for oc in range(OC2):
                    for k in range(OC1):
                        mm = pe.matmul(ps_tail[:, oc * GRAN:(oc + 1) * GRAN], w2s[:, k, oc * P:(oc + 1) * P], h1[:, k, :],
                                       start=(k == 0), stop=(k == OC1 - 1))
                mm.then_inc(h2_ps, 1)

            def layer3(gp):
                pe.wait_ge(h2_ready, upto(gp, 1, 1))
                for k in range(OC2):
                    mm = pe.matmul(ps_tail[0:1, 0:GRAN], sm[:, C_W3 + k:C_W3 + k + 1], h2[:, k, :],
                                   start=(k == 0), stop=(k == OC2 - 1))
                mm.then_inc(yo_ps, 1)

            def body(gp, back):
                transpose_rows(gp, 0, back)
                gram_rows(gp, 0)
                transpose_rows(gp, 1, back)
                project_fields(gp, 0, back)
                embed(gp, 0, back)
                if back:
                    pair_products(gp - 1, 1, True)
                gram_rows(gp, 1)
                if back:
                    project_pairs(gp - 1, 0, True)
                project_fields(gp, 1, back)
                embed(gp, 1, back)
                transpose_rows(gp, 2, back)
                if back:
                    project_pairs(gp - 1, 1, True)
                gram_rows(gp, 2)
                if back:
                    project_pairs(gp - 1, 2, True)
                project_fields(gp, 2, back)
                embed(gp, 2, back)
                transpose_rows(gp, 3, back)
                if back:
                    project_pairs(gp - 1, 3, True)
                gram_rows(gp, 3)
                if back:
                    sum_squares(gp - 1)
                project_fields(gp, 3, back)
                pair_products(gp, 0, back)
                if back:
                    layer1(gp - 1)
                embed(gp, 3, back)
                if back:
                    layer2(gp - 1)
                    layer3(gp - 1)

            pe.wait_ge(set_dve, 8)
            pe.wait_ge(set_act, 10)
            pe.wait_ge(ld_w2, 16)
            body(0, False)
            with pe.Fori(1, NG) as gp:
                body(gp, True)
            pair_products(NG - 1, 1, True)
            for lc in range(LC):
                project_pairs(NG - 1, lc, True)
            sum_squares(NG - 1)
            layer1(NG - 1)
            layer2(NG - 1)
            layer3(NG - 1)


def lay_out(inputs):
    import numpy as np
    a = {k: np.asarray(v) for k, v in inputs.items()}
    o = {}
    tables = [a[f"tbl_{f}"] for f in range(NF)]
    start = np.concatenate([[0], np.cumsum([t.shape[0] for t in tables])[:-1]]).astype(np.int32)

    flat = np.arange(TILES * P).reshape(TILES, P)
    bl, fld = flat // NF, flat % NF
    local = (bl // CB) * CHUNK + bl % CB
    b = (np.arange(NG)[:, None, None, None] * GRAN + local.T[None, :, :, None]
         + np.arange(2)[None, None, None, :] * CB)
    n = np.broadcast_to(fld.T[None, :, :, None], b.shape)
    o["ids"] = a["ids"][b, n].transpose(1, 0, 2, 3).reshape(P, -1)
    o["base"] = start[n].transpose(1, 0, 2, 3).reshape(P, -1)
    o["table"] = np.concatenate(tables, axis=0)

    ws = a["L0_rec_Ws"]
    o["ws_t"] = np.concatenate([ws.T, ws.T], axis=0)
    o["gs_row"] = np.broadcast_to(a["L0_rec_gs"], (P, E))
    o["ident"] = np.eye(P, dtype=np.float32)

    row_t = np.array([NPROJ] + list(range(1, NPROJ)))
    quad, r = np.divmod(np.arange(P), 32)
    ti = row_t[r]
    s = 1 + 8 * quad[:, None] + np.arange(KB)[None, :]
    is_x = s == X_SLOT
    tj = np.where(is_x, 0, s)
    gsi, bsi = a["L0_rec_gsi"], a["L0_rec_bsi"]
    sm = np.zeros((P, C_END), np.float32)
    sm[:, C_GD], sm[:, C_BD] = a["L0_rec_gd"], a["L0_rec_bd"]
    sm[:, C_GL:C_GL + LLIVE] = a["L0_rec_gl"][:LIVE].reshape(LLIVE, P).T
    sm[:, C_BL:C_BL + LLIVE] = a["L0_rec_bl"][:LIVE].reshape(LLIVE, P).T
    sm[:, C_B1:C_B1 + OC1] = a["b_top1"].reshape(OC1, P).T
    sm[:, C_B2:C_B2 + OC2] = a["b_top2"].reshape(OC2, P).T
    sm[:, C_W3:C_W3 + OC2] = a["W_top3"].reshape(OC2, P).T
    sm[:, C_GI], sm[:, C_BI] = gsi[ti - 1], bsi[ti - 1]
    sm[:, C_GJ:C_GJ + KB] = np.where(is_x, np.float32(1), gsi[tj - 1])
    sm[:, C_BJ:C_BJ + KB] = np.where(is_x, np.float32(0), bsi[tj - 1])
    sm[:, C_XM:C_XM + KB] = is_x
    o["small"] = sm
    pm = np.zeros((P, KB, 33), np.float32)
    pm[np.arange(P)[:, None], np.arange(KB)[None, :], np.where(is_x, 32, s)] = 1
    dl = np.zeros((P, 32), np.float32)
    dl[np.arange(P), r] = 1
    o["pair_mask"] = np.concatenate([pm.reshape(P, -1), dl], axis=1)

    wsi = a["L0_rec_Wsi"][row_t - 1]
    blocks = np.zeros((P, TILES, SPAN, NPROJ), np.float32)
    mask = np.zeros((P, TILES, SPAN, NPROJ), np.float16)
    for j in range(TILES):
        rows = np.arange(P)
        at = bl[j] - P * j // NF
        blocks[rows, j, at] = wsi.T[fld[j]]
        mask[rows, j, at] = 1
    o["wsi_blocks"] = blocks.reshape(P, TILES, SPAN * NPROJ)
    o["block_mask"] = mask.reshape(P, TILES, SPAN * NPROJ)
    o["wsi_small"] = wsi.T
    o["bs_rep"] = np.broadcast_to(a["L0_rec_bs"], (NF, E))

    o["wd_t"] = a["L0_rec_Wd"].T.reshape(2, P, E).transpose(1, 0, 2)
    o["dense_t"] = a["r_dense_t"].T.reshape(2, P, B).transpose(1, 0, 2)
    pair = ti[:, None] * (ti[:, None] - 1) // 2 + tj
    wl = np.zeros((P, KB, L), np.float32)
    keep = tj < ti[:, None]
    wl[keep] = a["L0_rec_Wl"].T[pair[keep]]
    o["wl_blocks"] = wl
    w1 = a["W_top1"]
    o["w1_z"] = w1[:LIVE].reshape(LLIVE, P, H1).transpose(1, 0, 2)
    o["w1_d"] = w1[L:].reshape(2, P, H1).transpose(1, 0, 2)
    o["w2"] = a["W_top2"].reshape(OC1, P, H2).transpose(1, 0, 2)
    return {k: np.ascontiguousarray(v) for k, v in o.items()}


def kernel(**inputs):
    import concourse.bacc as _bacc
    from concourse.bass_utils import run_bass_kernel_spmd as _run

    nc = _bacc.Bacc("TRN2", target_bir_lowering=False, num_devices=1)
    arrays, args = {}, {}
    for name, a in lay_out(inputs).items():
        arrays[f"in_{name}_dram"] = a
        args[name] = nc.dram_tensor(f"in_{name}_dram", a.shape, mybir.dt.from_np(a.dtype), kind="ExternalInput").ap()
    out = nc.dram_tensor("out_0_dram", (B, 1), F32, kind="ExternalOutput").ap()
    dlrm_tower(nc, **args, out=out)
    r = _run(nc, [arrays], core_ids=[0])
    return r.results[0]["out_0_dram"]
```

```python
from contextlib import ExitStack

import concourse.bass as bass
from concourse import mybir

F32 = mybir.dt.float32
I32 = mybir.dt.int32
ALU = mybir.AluOpType
ACT = mybir.ActivationFunctionType
AX_X = mybir.AxisListType.X

P = 128
B = 512
NF = 26
D = 64
E = 128
NPROJ = 32
DENSE = 256
L = 512
LIVE = 384
H1, H2 = 512, 256
EPS = 1e-5

GROUP = 64
GRAN = 2 * GROUP
HALF = GRAN // 2
NG = B // GRAN
TILES = GROUP * NF // P
BATCH_END = [4, 7, 10, 13]
NC = len(BATCH_END)
CB = GROUP // NC
CHUNK = 2 * CB
SPAN = 6
SLOTS = NPROJ + 2
X_SLOT, ONE_SLOT = NPROJ, NPROJ + 1
ZCOLS = NPROJ + 1
KB = 8
LC, LLIVE = L // P, LIVE // P
OC1, OC2 = H1 // P, H2 // P
ROW_ONE, ROW_X, ROW_S = 0, 32, 96
(C_GD, C_BD, C_GL, C_BL, C_B1, C_B2, C_W3, C_GI, C_BI, C_GJ, C_BJ, C_XM, C_END) = (
    0, 1, 2, 5, 8, 12, 14, 16, 17, 18, 26, 34, 42)


def batch(c):
    return range(BATCH_END[c - 1] if c else 0, BATCH_END[c])


def tile_spans(j):
    b0, b1 = P * j // NF, (P * j + P - 1) // NF + 1
    out = []
    while b0 < b1:
        end = min(b1, (b0 // CB + 1) * CB)
        out.append((b0 // CB, (b0 % CB) * NPROJ, (b0 - P * j // NF) * NPROJ, (end - b0) * NPROJ))
        b0 = end
    return out


def dlrm_tower(nc, ids, base, table, ws_t, gs_row, ident, small, pair_mask, wsi_rows, span_mask, wsi_small,
               bs_rep, wd_t, dense_t, wl_blocks, w1_z, w1_d, w2, out):
    with ExitStack() as ctx:
        def sb(name, shape, dt=F32):
            return ctx.enter_context(nc.sbuf_tensor(name, shape, dt))

        def sem(name):
            return ctx.enter_context(nc.semaphore(name))

        idx_in = sb("idx_in", [P, NG * 2 * TILES], I32)
        idx_base = sb("idx_base", [P, NG * 2 * TILES], I32)
        idx = sb("idx", [P, NG * 2 * TILES], I32)
        wc = sb("wc", [P, E])
        wc_nat = sb("wc_nat", [P, P])
        gram = sb("gram", [P, P])
        wcg = sb("wcg", [P, E])
        gs_sb = sb("gs_sb", [P, E])
        eye = sb("eye", [P, P])
        ones = sb("ones", [P, P])
        sm = sb("sm", [P, C_END])
        pmask = sb("pmask", [P, KB * 33 + 32])
        wrow = sb("wrow", [P, TILES, NPROJ])
        smask = sb("smask", [P, TILES, SPAN])
        S = sb("S", [P, TILES, SPAN, NPROJ])
        wmean = sb("wmean", [P, TILES])
        wsis = sb("wsis", [NF, NPROJ])
        bsr = sb("bsr", [NF, E])
        tiny = sb("tiny", [P, 16])
        bias_y = sb("bias_y", [P, NPROJ])
        wd = sb("wd", [P, 2, E])
        dns = sb("dns", [P, 2, B])
        wl = sb("wl", [P, KB + 1, L])
        kcoef = sb("kcoef", [P, 4 * KB])
        means = sb("means", [P, KB + 1])
        shift = sb("shift", [P, KB])
        scratch = sb("scratch", [P, KB + 1, L])
        dmat = sb("dmat", [P, KB, P])
        w1z = sb("w1z", [P, LLIVE, H1])
        w1d = sb("w1d", [P, 2, H1])
        w2s = sb("w2s", [P, OC1, H2])
        b1e = sb("b1e", [P, OC1])
        eps = sb("eps", [P, 1])
        warm = sb("warm", [P, 1])
        x_sb = sb("x_sb", [P, B])
        x_sq = sb("x_sq", [P, B])
        x_r = sb("x_r", [P, B])
        h1_dense = sb("h1_dense", [P, OC1, B])
        G = sb("G", [P, TILES, 2, D])
        gt = sb("gt", [P, 4 * P])
        qg = sb("qg", [P, 4 * P])
        var1 = sb("var1", [P, 8])
        sd1 = sb("sd1", [P, 8])
        r1 = sb("r1", [P, 8])
        ut = sb("ut", [P, 512])
        V = sb("V", [P, GRAN, SLOTS])
        sq2 = sb("sq2", [P, CHUNK, NPROJ])
        var2 = sb("var2", [P, CHUNK])
        sd2 = sb("sd2", [P, CHUNK])
        r2 = sb("r2", [P, CHUNK])
        zb = sb("zb", [P, KB, B])
        z8 = sb("z8", [P, B])
        f_sb = sb("f_sb", [P, LLIVE, GRAN])
        f_sq = sb("f_sq", [P, LC, GRAN])
        f_sum = sb("f_sum", [P, GRAN])
        sd3 = sb("sd3", [P, GRAN])
        r3 = sb("r3", [P, GRAN])
        zn = sb("zn", [P, LLIVE, GRAN])
        h1_pre = sb("h1_pre", [P, OC1, GRAN])
        h1 = sb("h1", [P, OC1, GRAN])
        h2 = sb("h2", [P, OC2, GRAN])
        h1_last = sb("h1_last", [P, OC1, GRAN])
        h2_last = sb("h2_last", [P, OC2, GRAN])
        y_row = sb("y_row", [1, B])
        ps_gq = ctx.enter_context(nc.psum_tensor("ps_gq", [P, 512], F32))
        ps_tail = ctx.enter_context(nc.psum_tensor("ps_tail", [P, 512], F32))
        ps_ut = ctx.enter_context(nc.psum_tensor("ps_ut", [P, 2, 512], F32))
        ps_y = ctx.enter_context(nc.psum_tensor("ps_y", [P, 2, 512], F32))
        ps_z = ctx.enter_context(nc.psum_tensor("ps_z", [P, 2, 512], F32))
        tail = ps_tail[:, :].rearrange("p (c b) -> p c b", b=GRAN)
        tail2 = ps_y[:, 0, :].rearrange("p (c b) -> p c b", b=GRAN)

        ld_ids, ld_wc, ld_ws, ld_wd, ld_pm, ld_sm, ld_s, ld_x, ld_w1z, ld_w1d, ld_w2 = [
            sem(n) for n in ("ld_ids", "ld_wc", "ld_ws", "ld_wd", "ld_pm", "ld_sm", "ld_s", "ld_x", "ld_w1z", "ld_w1d", "ld_w2")]
        ld_wl = [sem("ld_wl_a"), sem("ld_wl_b")]
        gathered = [sem(f"gathered{c}") for c in range(NC)]
        (idx_ready, consts_set, wc_ready, wcg_ready, wc_nat_ps, wc_nat_sb, gram_ps, gram_ready, patterns_ready, wsis_ready,
         bias_ps, bias_ready, wd_ready, xc_ps, x_sq_ready, xvar_ps, x_sd_ready, x_root, x_ready, xsum_ps, xsum_ready,
         b1_ps, b1_ready, dense_ps, dense_ready, w1_ready, ninth_in_ready, ninth_ps, ninth_mean, ninth_ready, wl_mean, wl_shift, wl_ready) = [
            sem(n) for n in (
                "idx_ready", "consts_set", "wc_ready", "wcg_ready", "wc_nat_ps", "wc_nat_sb", "gram_ps", "gram_ready",
                "patterns_ready", "wsis_ready", "bias_ps", "bias_ready", "wd_ready", "xc_ps", "x_sq_ready", "xvar_ps",
                "x_sd_ready", "x_root", "x_ready", "xsum_ps", "xsum_ready", "b1_ps", "b1_ready", "dense_ps", "dense_ready",
                "w1_ready", "ninth_in_ready", "ninth_ps", "ninth_mean", "ninth_ready", "wl_mean", "wl_shift", "wl_ready")]
        gt_ps, gt_sb, q_ps, q_used = sem("gt_ps"), sem("gt_sb"), sem("q_ps"), sem("q_used")
        var1_ready, sd1_ready, r1_ready, g_scaled = sem("var1_ready"), sem("sd1_ready"), sem("r1_ready"), sem("g_scaled")
        ut_ps, ut_sb, y_ps, y_sb = sem("ut_ps"), sem("ut_sb"), sem("y_ps"), sem("y_sb")
        sq_ready, var2_ready, sd2_ready, r2_ready, v_ready = (
            sem("sq_ready"), sem("var2_ready"), sem("sd2_ready"), sem("r2_ready"), sem("v_ready"))
        z_ps, z_sb = sem("z_ps"), sem("z_sb")
        f_ps, f_sq_ready, f_ready, f_sum_ready, ss_ps = (
            sem("f_ps"), sem("f_sq_ready"), sem("f_ready"), sem("f_sum_ready"), sem("ss_ps"))
        sd3_ready, r3_ready, zn_ready = sem("sd3_ready"), sem("r3_ready"), sem("zn_ready")
        h1_ps, h1_pre_ready, h1_ready, h2_ps, h2_ready = (
            sem("h1_ps"), sem("h1_pre_ready"), sem("h1_ready"), sem("h2_ps"), sem("h2_ready"))
        yo_ps, yo_ready, stored = sem("yo_ps"), sem("yo_ready"), sem("stored")

        def dense_bank(oc):
            return ps_z[:, oc, :] if oc < 2 else ps_tail[:, :]

        def chunk_v(c):
            return V[:, c * CHUNK:(c + 1) * CHUNK, 0:NPROJ]

        def nth(gp, c):
            return gp * NC + c + 1

        def nth_half(gp, h):
            return gp * 2 + h + 1


        block = ctx.enter_context(nc.Block())

        @block.sync
        def _(sp):
            sp.dma_start(idx_in[:, :], ids).then_inc(ld_ids, 16)
            sp.dma_start(idx_base[:, :], base).then_inc(ld_ids, 16)
            sp.dma_start(wsis[:, :], wsi_small).then_inc(ld_s, 16)
            sp.dma_start(bsr[:, :], bs_rep).then_inc(ld_s, 16)
            sp.dma_start(wrow[:, :, :], wsi_rows).then_inc(ld_s, 16)
            sp.dma_start(smask[:, :, :], span_mask).then_inc(ld_s, 16)
            sp.dma_start(sm[:, :], small).then_inc(ld_sm, 16)
            sp.dma_start(w1z[:, :, :], w1_z).then_inc(ld_w1z, 16)
            sp.wait_ge(gathered[0], 2 * len(batch(0)) * 16)
            sp.dma_start(pmask[:, :], pair_mask).then_inc(ld_pm, 16)
            sp.dma_start(w1d[:, :, :], w1_d).then_inc(ld_w1d, 16)
            for h in range(2):
                sp.wait_ge(gathered[1 + h], 2 * len(batch(1 + h)) * 16)
                k = h * KB // 2
                sp.dma_start(wl[:, k:k + KB // 2, :], wl_blocks[:, k:k + KB // 2, :]).then_inc(ld_wl[h], 16)
            sp.wait_ge(gathered[3], 2 * len(batch(3)) * 16)
            sp.dma_start(w2s[:, :, :], w2).then_inc(ld_w2, 16)
            sp.wait_ge(yo_ready, NG)
            sp.dma_start(out.rearrange("b o -> o b"), y_row[:, :]).then_inc(stored, 16)
            sp.wait_ge(stored, 16)

        @block.gpsimd
        def _(pool):
            pool.wait_ge(idx_ready, 1)
            for gp in range(NG):
                for c in range(NC):
                    if gp:
                        pool.wait_ge(ut_ps, nth(gp - 1, c))
                    for j in batch(c):
                        for g in range(2):
                            k = gp * 2 * TILES + 2 * j + g
                            pool.indirect_dma_start(
                                G[:, j, g, :], None, table,
                                bass.IndirectOffsetOnAxis(ap=idx[:, k:k + 1], axis=0)).then_inc(gathered[c], 16)

        @block.scalar
        def _(act):
            act.dma_start(wc[:, :], ws_t).then_inc(ld_wc, 16)
            act.dma_start(wd[:, :, :], wd_t).then_inc(ld_wd, 16)
            act.dma_start(dns[:, :, :], dense_t).then_inc(ld_x, 16)
            act.wait_ge(consts_set, 1)
            act.activation(warm[:, :], eps[:, :], ACT.Sqrt)
            act.dma_start(eye[:, :], ident).then_inc(ld_ws, 16)
            act.dma_start(gs_sb[:, :], gs_row).then_inc(ld_ws, 16)

            def prepare_embedding():
                act.wait_ge(wc_nat_ps, 1)
                act.copy(wc_nat[:, :], ps_ut[:, 0, 0:P]).then_inc(wc_nat_sb, 1)
                act.wait_ge(bias_ps, 1)
                act.copy(bias_y[:, :], ps_y[:, 0, 0:NPROJ]).then_inc(bias_ready, 1)

            def prepare_x():
                act.wait_ge(xc_ps, 1)
                act.activation(x_sq[:, :], ps_y[:, 1, :], ACT.Square).then_inc(x_sq_ready, 1)
                act.wait_ge(xvar_ps, 1)
                act.wait_ge(consts_set, 1)
                act.activation(x_r[:, :], ps_z[:, 0, :], ACT.Sqrt, bias=eps[:, :], scale=1.0 / E).then_inc(x_sd_ready, 1)

            def prepare_dense(oc):
                act.wait_ge(b1_ready, 1)
                act.wait_ge(dense_ps, oc + 1)
                act.activation(h1_dense[:, oc, :], dense_bank(oc), ACT.Identity, bias=b1e[:, oc:oc + 1]).then_inc(dense_ready, 1)

            def prepare_means(h):
                act.wait_ge(ld_wl[h], 16)
                for k in range(h * KB // 2, (h + 1) * KB // 2):
                    last = act.activation(scratch[:, k, :], wl[:, k, :], ACT.Identity, scale=-1.0 / L, accum_out=means[:, k:k + 1])
                last.then_inc(wl_mean, 1)

            def prepare_xsum():
                act.wait_ge(xsum_ps, 1)
                act.copy(z8[ROW_X:ROW_X + 1, :], ps_tail[ROW_X:ROW_X + 1, :]).then_inc(xsum_ready, 1)

            def prepare_ninth():
                act.wait_ge(ninth_ps, 1)
                act.activation(scratch[:, KB, :], ps_tail[:, :], ACT.Identity, scale=-1.0 / L,
                               accum_out=means[:, KB:KB + 1]).then_inc(ninth_mean, 1)
                act.wait_ge(ninth_mean, 1)
                act.activation(wl[:, KB, :], ps_tail[:, :], ACT.Identity, bias=means[:, KB:KB + 1]).then_inc(ninth_ready, 1)

            def prepare_gains(start, end):
                act.wait_ge(ninth_ps, 1)
                act.wait_ge(wl_shift, 1)
                for k in range(start, end):
                    last = act.activation(wl[:, k, :], wl[:, k, :], ACT.Identity, bias=shift[:, k:k + 1],
                                          scale=kcoef[:, 3 * KB + k:3 * KB + k + 1])
                last.then_inc(wl_ready, 1)

            def gt_copy(gp, c):
                n = len(batch(c)) * P
                act.wait_ge(gt_ps, nth(gp, c))
                act.copy(gt[:, 0:n], ps_gq[:, 0:n]).then_inc(gt_sb, 1)

            def deviation1(gp, c):
                n = len(batch(c)) * 2
                act.wait_ge(var1_ready, nth(gp, c))
                act.activation(sd1[:, 0:n], var1[:, 0:n], ACT.Sqrt, bias=eps[:, :], scale=1.0 / E).then_inc(sd1_ready, 1)

            def ut_copy(gp, c):
                act.wait_ge(ut_ps, nth(gp, c))
                act.copy(ut[:, :], ps_ut[:, c % 2, :]).then_inc(ut_sb, 1)

            def square2(gp, c):
                act.wait_ge(y_sb, 2 * nth(gp, c))
                act.activation(sq2[:, :, :], chunk_v(c), ACT.Square).then_inc(sq_ready, 1)

            def deviation2(gp, c):
                act.wait_ge(var2_ready, nth(gp, c))
                act.activation(sd2[:, :], var2[:, :], ACT.Sqrt, bias=eps[:, :], scale=1.0 / NPROJ).then_inc(sd2_ready, 1)

            def z_copy(gp, h, quadrants):
                act.wait_ge(z_ps, nth_half(gp, h))
                for qb in quadrants:
                    src = ps_z[32 * qb:32 * qb + 32, :, 0:8 * ZCOLS].rearrange("p w (b c) -> p w b c", c=ZCOLS)
                    b0 = h * HALF + 16 * qb
                    for q in range(4):
                        dst = zb[32 * q:32 * q + 32, :, bass.ds(gp * GRAN + b0, 16)].rearrange("p k (w b) -> p w b k", w=2)
                        act.copy(dst, src[:, :, :, 8 * q:8 * q + 8])
                    last = act.copy(z8[ROW_S:ROW_S + 32, bass.ds(gp * GRAN + b0, 16)].rearrange("p (w b) -> p w b", w=2),
                                    src[:, :, :, ZCOLS - 1])
                last.then_inc(z_sb, 1)

            def f_squares(gp, bank=tail):
                act.wait_ge(f_ps, gp + 1)
                act.activation(f_sq[:, :, :], bank, ACT.Square).then_inc(f_sq_ready, 1)

            def f_copy(gp, bank=tail):
                act.copy(f_sb[:, :, :], bank[:, 0:LLIVE, :]).then_inc(f_ready, 1)

            def deviation3(gp, bank=tail):
                act.wait_ge(ss_ps, gp + 1)
                act.activation(sd3[:, :], bank[:, 0, :], ACT.Sqrt, bias=eps[:, :], scale=1.0 / L).then_inc(sd3_ready, 1)

            def relu1(gp, into=h1):
                act.wait_ge(h1_pre_ready, gp + 1)
                act.activation(into[:, :, :], h1_pre[:, :, :], ACT.Relu).then_inc(h1_ready, 1)

            def relu2(gp, bank=tail, into=h2):
                act.wait_ge(h2_ps, gp + 1)
                for oc in range(OC2):
                    last = act.activation(into[:, oc, :], bank[:, oc, :], ACT.Relu, bias=sm[:, C_B2 + oc:C_B2 + oc + 1])
                last.then_inc(h2_ready, 1)

            def y_copy(gp, bank=tail):
                act.wait_ge(yo_ps, gp + 1)
                act.copy(y_row[:, bass.ds(gp * GRAN, GRAN)], bank[0:1, 0, :]).then_inc(yo_ready, 1)

            def slots01(gp, before=2):
                gt_copy(gp, 1)
                if before == 2:
                    f_squares(gp - 2)
                ut_copy(gp, 0)
                deviation2(gp - 1, 3)
                if before == 2:
                    f_copy(gp - 2)
                z_copy(gp - 1, 0, (2, 3))
                deviation1(gp, 1)
                if before == 2:
                    deviation3(gp - 2)
                if before == 1:
                    prepare_gains(3, 6)
                square2(gp, 0)
                if before == 1:
                    prepare_dense(2)

                gt_copy(gp, 2)
                if before == 2:
                    relu1(gp - 2)
                ut_copy(gp, 1)
                deviation2(gp, 0)
                z_copy(gp - 1, 1, (0, 1))
                deviation1(gp, 2)
                if before == 2:
                    relu2(gp - 2)
                z_copy(gp - 1, 1, (2, 3))
                if before == 2:
                    y_copy(gp - 2)
                if before == 1:
                    prepare_gains(6, KB)
                    prepare_dense(3)

            def slots23(gp, before=2):
                gt_copy(gp, 3)
                ut_copy(gp, 2)
                square2(gp, 1)
                deviation1(gp, 3)
                deviation2(gp, 1)
                if not before:
                    prepare_means(1)
                square2(gp, 2)

                gt_copy(gp + 1, 0)
                ut_copy(gp, 3)
                deviation2(gp, 2)
                if not before:
                    prepare_ninth()
                deviation1(gp + 1, 0)
                if not before:
                    prepare_gains(0, 3)
                square2(gp, 3)
                z_copy(gp, 0, (0, 1))

            def last_slots(gp):
                gt_copy(gp, 3)
                ut_copy(gp, 2)
                square2(gp, 1)
                deviation1(gp, 3)
                deviation2(gp, 1)
                ut_copy(gp, 3)
                square2(gp, 2)
                deviation2(gp, 2)
                square2(gp, 3)
                z_copy(gp, 0, (0, 1))
                deviation2(gp, 3)
                z_copy(gp, 0, (2, 3))
                z_copy(gp, 1, (0, 1))
                f_squares(gp - 1)
                f_copy(gp - 1)
                deviation3(gp - 1)
                f_squares(gp, tail2)
                act.wait_ge(zn_ready, gp)
                f_copy(gp, tail2)
                deviation3(gp, tail2)
                relu1(gp - 1)
                relu1(gp, h1_last)
                relu2(gp - 1)
                relu2(gp, tail2, h2_last)
                y_copy(gp - 1)
                y_copy(gp, tail2)

            prepare_embedding()
            prepare_x()
            gt_copy(0, 0)
            deviation1(0, 0)
            gt_copy(0, 1)
            ut_copy(0, 0)
            deviation1(0, 1)
            square2(0, 0)
            prepare_xsum()
            prepare_dense(0)
            gt_copy(0, 2)
            ut_copy(0, 1)
            deviation2(0, 0)
            deviation1(0, 2)
            prepare_means(0)
            prepare_dense(1)
            slots23(0, before=0)
            slots01(1, before=1)
            with act.Fori(1, NG - 1) as gp:
                slots23(gp)
                slots01(gp + 1)
            last_slots(NG - 1)

        @block.vector
        def _(dve):
            chain = sem("dve_chain")
            count = [0]

            def link(ins):
                count[0] += 1
                ins.then_inc(chain, 1)
                dve.wait_ge(chain, count[0])

            def prepare_embedding():
                dve.wait_ge(ld_ids, 32)
                dve.tensor_tensor(idx[:, :], idx_in[:, :], idx_base[:, :], ALU.add).then_inc(idx_ready, 1)
                dve.wait_ge(ld_wc, 16)
                link(dve.reduce_sum(tiny[:, 0:1], wc[:, :], AX_X))
                link(dve.tensor_scalar(tiny[:, 0:1], tiny[:, 0:1], -1.0 / E, None, ALU.mult))
                dve.tensor_scalar(wc[:, :], wc[:, :], tiny[:, 0:1], None, ALU.add).then_inc(wc_ready, 1)

            def prepare_gram():
                dve.wait_ge(gram_ps, 1)
                for h in (0, 64):
                    last = dve.tensor_copy(gram[h:h + 64, h:h + 64], ps_ut[h:h + 64, 1, h:h + 64])
                last.then_inc(gram_ready, 1)
                dve.wait_ge(ld_ws, 32)
                dve.tensor_tensor(wcg[:, :], wc[:, :], gs_sb[:, :], ALU.mult).then_inc(wcg_ready, 1)

            def prepare_wsis():
                dve.wait_ge(ld_s, 64)
                link(dve.reduce_sum(tiny[0:NF, 1:2], wsis[:, :], AX_X))
                link(dve.tensor_scalar(tiny[0:NF, 1:2], tiny[0:NF, 1:2], -1.0 / NPROJ, None, ALU.mult))
                dve.tensor_scalar(wsis[:, :], wsis[:, :], tiny[0:NF, 1:2], None, ALU.add).then_inc(wsis_ready, 1)

            def prepare_wd():
                dve.wait_ge(ld_wd, 16)
                link(dve.reduce_sum(tiny[:, 2:4], wd[:, :, :], AX_X))
                link(dve.tensor_scalar(tiny[:, 2:4], tiny[:, 2:4], -1.0 / E, None, ALU.mult))
                for k in range(2):
                    last = dve.tensor_scalar(wd[:, k, :], wd[:, k, :], tiny[:, 2 + k:3 + k], None, ALU.add)
                last.then_inc(wd_ready, 1)

            def prepare_constants():
                dve.memset(eps[:, :], EPS).then_inc(consts_set, 1)
                dve.memset(gram[:, :], 0.0)
                dve.memset(ones[:, :], 1.0)
                dve.memset(dmat[:, :, :], 0.0)
                dve.memset(V[:, :, ONE_SLOT], 1.0)
                link(dve.memset(z8[:, :], 0.0))
                dve.memset(z8[ROW_ONE:ROW_ONE + 1, :], 1.0).then_inc(consts_set, 1)

            def prepare_patterns():
                link(dve.reduce_sum(wmean[:, :], wrow[:, :, :], AX_X))
                link(dve.tensor_scalar(wmean[:, :], wmean[:, :], -1.0 / NPROJ, None, ALU.mult))
                link(dve.tensor_tensor(wrow[:, :, :], wrow[:, :, :],
                                       wmean[:, :].unsqueeze(2).broadcast_to([P, TILES, NPROJ]), ALU.add))
                dve.tensor_tensor(S[:, :, :, :], wrow[:, :, :].unsqueeze(2).broadcast_to([P, TILES, SPAN, NPROJ]),
                                  smask[:, :, :].unsqueeze(3).broadcast_to([P, TILES, SPAN, NPROJ]),
                                  ALU.mult).then_inc(patterns_ready, 1)

            def prepare_b1():
                dve.wait_ge(ld_sm, 16)
                dve.wait_ge(b1_ps, 1)
                dve.tensor_tensor(b1e[:, :], ps_tail[:, 0:OC1], sm[:, C_B1:C_B1 + OC1], ALU.add).then_inc(b1_ready, 1)

            def prepare_w1():
                for k in range(LLIVE):
                    last = dve.tensor_scalar(w1z[:, k, :], w1z[:, k, :], sm[:, C_GL + k:C_GL + k + 1], None, ALU.mult)
                last.then_inc(w1_ready, 1)

            def prepare_x_root(h):
                if h == 0:
                    dve.wait_ge(x_sd_ready, 1)
                dve.reciprocal(x_sq[:, h * B // 2:(h + 1) * B // 2], x_r[:, h * B // 2:(h + 1) * B // 2]).then_inc(x_root, 1)

            def prepare_x():
                dve.wait_ge(ld_sm, 16)
                dve.wait_ge(x_root, 2)
                link(dve.tensor_tensor(x_sb[:, :], ps_y[:, 1, :], x_sq[:, :], ALU.mult))
                dve.tensor_scalar(x_sb[:, :], x_sb[:, :], sm[:, C_GD:C_GD + 1], sm[:, C_BD:C_BD + 1],
                                  ALU.mult, ALU.add).then_inc(x_ready, 1)

            def prepare_ninth():
                dve.wait_ge(ld_pm, 16)
                gj, bj = (sm[:, c:c + KB] for c in (C_GJ, C_BJ))
                gi, bi = sm[:, C_GI:C_GI + 1], sm[:, C_BI:C_BI + 1]
                k_gb, k_bg, k_bb, k_gg = (kcoef[:, n * KB:(n + 1) * KB] for n in range(4))
                dve.tensor_scalar(k_gb, bj, gi, None, ALU.mult)
                dve.tensor_scalar(k_bg, gj, bi, None, ALU.mult)
                dve.tensor_scalar(k_bb, bj, bi, float(E), ALU.mult, ALU.mult)
                link(dve.tensor_scalar(k_gg, gj, gi, None, ALU.mult))
                pm = pmask[:, 0:KB * 33].rearrange("p (k c) -> p k c", c=33)
                delta = pmask[:, KB * 33:KB * 33 + 32]
                dve.tensor_tensor(dmat[:, :, ROW_X], pm[:, :, 32], k_bg, ALU.mult)
                dve.tensor_copy(dmat[:, :, ROW_ONE], k_bb)
                link(dve.tensor_tensor(dmat[:, :, ROW_S:ROW_S + 32], pm[:, :, 0:32],
                                       k_bg.unsqueeze(2).broadcast_to([P, KB, 32]), ALU.mult))
                for k in range(KB):
                    last = dve.scalar_tensor_tensor(dmat[:, k, ROW_S:ROW_S + 32], delta, k_gb[:, k:k + 1],
                                                    dmat[:, k, ROW_S:ROW_S + 32], ALU.mult, ALU.add)
                last.then_inc(ninth_in_ready, 1)

            def prepare_shift():
                dve.wait_ge(wl_mean, 2)
                dve.tensor_tensor(shift[:, :], means[:, 0:KB], kcoef[:, 3 * KB:4 * KB], ALU.mult).then_inc(wl_shift, 1)

            def variance1(gp, c):
                js = batch(c)
                n = len(js)
                dve.wait_ge(q_ps, nth(gp, c))
                dve.tensor_tensor(qg[:, 0:n * P], ps_gq[:, 0:n * P],
                                  G[:, js[0]:js[0] + n, :, :].rearrange("p j g d -> p (j g d)"),
                                  ALU.mult).then_inc(q_used, 1)
                dve.wait_ge(q_used, nth(gp, c))
                dve.reduce_sum(var1[:, 0:2 * n], qg[:, 0:n * P].rearrange("p (t d) -> p t d", d=D), AX_X).then_inc(var1_ready, 1)

            def scale_rows(gp, c):
                js = batch(c)
                n = 2 * len(js)
                dve.wait_ge(sd1_ready, nth(gp, c))
                dve.reciprocal(r1[:, 0:n], sd1[:, 0:n]).then_inc(r1_ready, 1)
                dve.wait_ge(r1_ready, nth(gp, c))
                rows = G[:, js[0]:js[0] + n // 2, :, :].rearrange("p j g d -> p (j g) d")
                dve.tensor_tensor(rows, rows, r1[:, 0:n].unsqueeze(2).broadcast_to([P, n, D]), ALU.mult).then_inc(g_scaled, 1)

            def x_slots(gp, h):
                dve.tensor_copy(V[:, h * HALF:(h + 1) * HALF, X_SLOT], x_sb[:, bass.ds(gp * GRAN + h * HALF, HALF)])

            def y_evacuate(gp, c):
                for g in range(2):
                    dve.wait_ge(y_ps, 2 * nth(gp, c) - 1 + g)
                    b0 = c * CHUNK + g * CB
                    dve.tensor_tensor(V[:, b0:b0 + CB, 0:NPROJ], ps_y[:, g, :].rearrange("p (b q) -> p b q", q=NPROJ),
                                      bias_y[:, :].unsqueeze(1).broadcast_to([P, CB, NPROJ]), ALU.add).then_inc(y_sb, 1)

            def variance2(gp, c):
                dve.wait_ge(sq_ready, nth(gp, c))
                dve.reduce_sum(var2[:, :], sq2[:, :, :], AX_X).then_inc(var2_ready, 1)

            def normalise2(gp, c):
                dve.wait_ge(sd2_ready, nth(gp, c))
                dve.reciprocal(r2[:, :], sd2[:, :]).then_inc(r2_ready, 1)
                dve.wait_ge(r2_ready, nth(gp, c))
                dve.tensor_tensor(chunk_v(c), chunk_v(c), r2[:, :].unsqueeze(2).broadcast_to([P, CHUNK, NPROJ]),
                                  ALU.mult).then_inc(v_ready, 1)

            def sum_blocks3(gp):
                dve.wait_ge(f_sq_ready, gp + 1)
                dve.reduce_sum(f_sum[:, :], f_sq[:, :, :].rearrange("p c b -> p b c"), AX_X).then_inc(f_sum_ready, 1)

            def normalise3(gp):
                dve.wait_ge(sd3_ready, gp + 1)
                dve.reciprocal(r3[:, :], sd3[:, :]).then_inc(r3_ready, 1)
                dve.wait_ge(r3_ready, gp + 1)
                dve.tensor_tensor(zn[:, :, :], f_sb[:, :, :], r3[:, :].unsqueeze(1).broadcast_to([P, LLIVE, GRAN]),
                                  ALU.mult).then_inc(zn_ready, 1)

            def add_dense(gp, bank=tail):
                dve.wait_ge(h1_ps, gp + 1)
                dve.tensor_tensor(h1_pre[:, :, :], bank, h1_dense[:, :, bass.ds(gp * GRAN, GRAN)],
                                  ALU.add).then_inc(h1_pre_ready, 1)

            def slots01(gp, before=2):
                if before == 2:
                    sum_blocks3(gp - 2)
                variance1(gp, 1)
                normalise2(gp - 1, 3)
                if before == 2:
                    normalise3(gp - 2)
                scale_rows(gp, 1)
                dve.wait_ge(z_ps, nth_half(gp - 1, 0))
                x_slots(gp, 0)
                y_evacuate(gp, 0)

                if before == 2:
                    add_dense(gp - 2)
                variance2(gp, 0)
                if before == 1:
                    prepare_w1()
                variance1(gp, 2)
                normalise2(gp, 0)
                scale_rows(gp, 2)
                y_evacuate(gp, 1)

            def slots23(gp, before=2):
                variance1(gp, 3)
                variance2(gp, 1)
                scale_rows(gp, 3)
                normalise2(gp, 1)
                if before:
                    dve.wait_ge(z_ps, nth_half(gp - 1, 1))
                x_slots(gp, 1)
                y_evacuate(gp, 2)
                variance2(gp, 2)

                if not before:
                    prepare_shift()
                variance1(gp + 1, 0)
                normalise2(gp, 2)
                y_evacuate(gp, 3)
                scale_rows(gp + 1, 0)
                variance2(gp, 3)

            def z_copy(gp, h, quadrants):
                dve.wait_ge(z_ps, nth_half(gp, h))
                for qb in quadrants:
                    src = ps_z[32 * qb:32 * qb + 32, :, 0:8 * ZCOLS].rearrange("p w (b c) -> p w b c", c=ZCOLS)
                    b0 = gp * GRAN + h * HALF + 16 * qb
                    for q in range(4):
                        dst = zb[32 * q:32 * q + 32, :, b0:b0 + 16].rearrange("p k (w b) -> p w b k", w=2)
                        dve.tensor_copy(dst, src[:, :, :, 8 * q:8 * q + 8])
                    last = dve.tensor_copy(z8[ROW_S:ROW_S + 32, b0:b0 + 16].rearrange("p (w b) -> p w b", w=2),
                                           src[:, :, :, ZCOLS - 1])
                last.then_inc(z_sb, 1)

            def last_slots(gp):
                variance1(gp, 3)
                variance2(gp, 1)
                scale_rows(gp, 3)
                normalise2(gp, 1)
                dve.wait_ge(z_ps, nth_half(gp - 1, 1))
                x_slots(gp, 1)
                y_evacuate(gp, 2)
                variance2(gp, 2)
                y_evacuate(gp, 3)
                normalise2(gp, 2)
                variance2(gp, 3)
                normalise2(gp, 3)
                z_copy(gp, 1, (2, 3))
                sum_blocks3(gp - 1)
                normalise3(gp - 1)
                sum_blocks3(gp)
                add_dense(gp - 1)
                normalise3(gp)
                dve.wait_ge(h1_ready, gp)
                add_dense(gp, tail2)

            prepare_constants()
            prepare_embedding()
            prepare_wd()
            prepare_wsis()
            prepare_gram()
            prepare_patterns()
            prepare_x_root(0)
            variance1(0, 0)
            scale_rows(0, 0)
            prepare_x_root(1)
            prepare_x()
            variance1(0, 1)
            scale_rows(0, 1)
            prepare_b1()
            x_slots(0, 0)
            dve.wait_ge(bias_ready, 1)
            y_evacuate(0, 0)
            variance2(0, 0)
            variance1(0, 2)
            normalise2(0, 0)
            scale_rows(0, 2)
            y_evacuate(0, 1)
            prepare_ninth()
            slots23(0, before=0)
            slots01(1, before=1)
            with dve.Fori(1, NG - 1) as gp:
                slots23(gp)
                slots01(gp + 1)
            last_slots(NG - 1)

        @block.tensor
        def _(pe):
            def prepare_embedding():
                pe.wait_ge(ld_ws, 32)
                pe.wait_ge(wc_ready, 1)
                pe.transpose(ps_ut[:, 0, 0:P], wc[:, :], eye[:, :]).then_inc(wc_nat_ps, 1)
                pe.wait_ge(wc_nat_sb, 1)
                pe.matmul(ps_ut[:, 1, 0:P], wc_nat[:, :], wc_nat[:, :], start=True, stop=True).then_inc(gram_ps, 1)
                pe.wait_ge(wsis_ready, 1)
                pe.wait_ge(ld_s, 64)
                pe.matmul(ps_y[:, 0, 0:NPROJ], bsr[:, :], wsis[:, :], start=True, stop=True).then_inc(bias_ps, 1)

            def prepare_x():
                pe.wait_ge(wd_ready, 1)
                pe.wait_ge(ld_x, 16)
                for k in range(2):
                    mm = pe.matmul(ps_y[:, 1, :], wd[:, k, :], dns[:, k, :], start=(k == 0), stop=(k == 1))
                mm.then_inc(xc_ps, 1)
                pe.wait_ge(x_sq_ready, 1)
                pe.wait_ge(consts_set, 2)
                pe.matmul(ps_z[:, 0, :], ones[:, :], x_sq[:, :], start=True, stop=True).then_inc(xvar_ps, 1)

            def prepare_b1():
                pe.wait_ge(ld_w1z, 16)
                pe.wait_ge(ld_sm, 16)
                for oc in range(OC1):
                    for k in range(LLIVE):
                        mm = pe.matmul(ps_tail[:, oc:oc + 1], w1z[:, k, oc * P:(oc + 1) * P],
                                       sm[:, C_BL + k:C_BL + k + 1], start=(k == 0), stop=(k == LLIVE - 1))
                mm.then_inc(b1_ps, 1)

            def prepare_dense(oc):
                pe.wait_ge(ld_w1d, 16)
                if oc == 0:
                    pe.wait_ge(x_sd_ready, 1)
                if oc == 2:
                    pe.wait_ge(ninth_ready, 1)
                if oc == 3:
                    pe.wait_ge(dense_ready, 3)
                for k in range(2):
                    mm = pe.matmul(dense_bank(oc), w1d[:, k, oc * P:(oc + 1) * P], dns[:, k, :],
                                   start=(k == 0), stop=(k == 1))
                mm.then_inc(dense_ps, 1)

            def prepare_xsum():
                pe.wait_ge(b1_ready, 1)
                pe.matmul(ps_tail[ROW_X:ROW_X + 1, :], ones[:, 0:1], x_sb[:, :], start=True, stop=True).then_inc(xsum_ps, 1)

            def prepare_ninth():
                for loaded in ld_wl:
                    pe.wait_ge(loaded, 16)
                pe.wait_ge(ninth_in_ready, 1)
                pe.wait_ge(xsum_ready, 1)
                for k in range(KB):
                    mm = pe.matmul(ps_tail[:, :], dmat[:, k, :], wl[:, k, :], start=(k == 0), stop=(k == KB - 1))
                mm.then_inc(ninth_ps, 1)

            def transpose_rows(gp, c, first=False):
                js = batch(c)
                pe.wait_ge(gathered[c], (gp + 1) * 2 * len(js) * 16)
                if not first:
                    pe.wait_ge(q_used, nth(gp, c) - 1)
                for n, j in enumerate(js):
                    mm = pe.transpose(ps_gq[:, n * P:(n + 1) * P], G[:, j, :, :].rearrange("p g d -> p (g d)"), eye[:, :])
                mm.then_inc(gt_ps, 1)

            def gram_rows(gp, c):
                pe.wait_ge(gt_sb, nth(gp, c))
                for n in range(len(batch(c))):
                    mm = pe.matmul(ps_gq[:, n * P:(n + 1) * P], gt[:, n * P:(n + 1) * P], gram[:, :], start=True, stop=True)
                mm.then_inc(q_ps, 1)

            def project_fields(gp, c, first=False):
                pe.wait_ge(g_scaled, nth(gp, c))
                if not first:
                    pe.wait_ge(ut_sb, nth(gp, c) - 1)
                for j in batch(c):
                    for chunk, col, scol, n in tile_spans(j):
                        begins = (P * j // NF) // CB != chunk or (P * j) % (CB * NF) == 0
                        mm = pe.matmul(ps_ut[:, chunk % 2, col:col + n], G[:, j, :, :].rearrange("p g d -> p (g d)"),
                                       S[:, j, :, :].rearrange("p s q -> p (s q)")[:, scol:scol + n],
                                       start=begins, stop=True, skip_group_check=True)
                mm.then_inc(ut_ps, 1)

            def embed(gp, c, first=False):
                pe.wait_ge(ut_sb, nth(gp, c))
                for g in range(2):
                    if not first:
                        pe.wait_ge(y_sb, 2 * nth(gp, c) - 3 + g)
                    pe.matmul(ps_y[:, g, :], wcg[64 * g:64 * g + 64, :], ut[64 * g:64 * g + 64, :],
                              start=True, stop=True).then_inc(y_ps, 1)

            def pair_products(gp, h, first=False):
                pe.wait_ge(v_ready, nth(gp, 2 * h + 1))
                if first:
                    pe.wait_ge(dense_ready, 2)
                else:
                    pe.wait_ge(z_sb, 2 * nth_half(gp, h) - 2)
                for bb in range(16):
                    for qb in range(4):
                        b = h * HALF + 16 * qb + bb
                        col = (bb % 8) * ZCOLS
                        mm = pe.matmul(ps_z[32 * qb:32 * qb + 32, bb // 8, col:col + ZCOLS], V[:, b, 0:NPROJ],
                                       V[:, b, 1:SLOTS], start=True, stop=True)
                mm.then_inc(z_ps, 1)

            def project_pairs(gp, lcs, bank=tail):
                if lcs[0] == 0:
                    pe.wait_ge(wl_ready, 3)
                    pe.wait_ge(dense_ready, OC1)
                    pe.wait_ge(z_sb, 2 * nth_half(gp, 1))
                for lc in lcs:
                    for k in range(KB + 1):
                        rhs = (zb[:, k, :] if k < KB else z8[:, :])[:, bass.ds(gp * GRAN, GRAN)]
                        mm = pe.matmul(bank[:, lc, :], wl[:, k, lc * P:(lc + 1) * P], rhs, start=(k == 0), stop=(k == KB))
                if lcs[-1] == LC - 1:
                    mm.then_inc(f_ps, 1)

            def sum_squares(gp, bank=tail):
                pe.wait_ge(f_sum_ready, gp + 1)
                pe.wait_ge(f_ready, gp + 1)
                pe.matmul(bank[:, 0, :], ones[:, :], f_sum[:, :], start=True, stop=True).then_inc(ss_ps, 1)

            def layer1(gp, bank=tail):
                pe.wait_ge(w1_ready, 1)
                pe.wait_ge(zn_ready, gp + 1)
                for oc in range(OC1):
                    for k in range(LLIVE):
                        mm = pe.matmul(bank[:, oc, :], w1z[:, k, oc * P:(oc + 1) * P], zn[:, k, :],
                                       start=(k == 0), stop=(k == LLIVE - 1))
                mm.then_inc(h1_ps, 1)

            def layer2(gp, bank=tail, h=h1):
                pe.wait_ge(ld_w2, 16)
                pe.wait_ge(h1_ready, gp + 1)
                for oc in range(OC2):
                    for k in range(OC1):
                        mm = pe.matmul(bank[:, oc, :], w2s[:, k, oc * P:(oc + 1) * P], h[:, k, :],
                                       start=(k == 0), stop=(k == OC1 - 1))
                mm.then_inc(h2_ps, 1)

            def layer3(gp, bank=tail, h=h2):
                pe.wait_ge(h2_ready, gp + 1)
                for k in range(OC2):
                    mm = pe.matmul(bank[0:1, 0, :], sm[:, C_W3 + k:C_W3 + k + 1], h[:, k, :],
                                   start=(k == 0), stop=(k == OC2 - 1))
                mm.then_inc(yo_ps, 1)

            def slots01(gp, before=2):
                transpose_rows(gp, 1)
                project_fields(gp, 0)
                gram_rows(gp, 1)
                embed(gp, 0)
                if before == 2:
                    sum_squares(gp - 2)
                pair_products(gp - 1, 1)
                if before == 1:
                    prepare_dense(2)
                if before == 2:
                    layer1(gp - 2)

                transpose_rows(gp, 2)
                project_fields(gp, 1)
                gram_rows(gp, 2)
                if before == 2:
                    layer2(gp - 2)
                embed(gp, 1)
                if before == 1:
                    prepare_dense(3)
                if before == 2:
                    layer3(gp - 2)

            def slots23(gp, before=2):
                transpose_rows(gp, 3)
                project_fields(gp, 2)
                gram_rows(gp, 3)
                embed(gp, 2)
                if before:
                    project_pairs(gp - 1, (0, 1, 2))
                else:
                    prepare_ninth()

                transpose_rows(gp + 1, 0)
                project_fields(gp, 3)
                gram_rows(gp + 1, 0)
                embed(gp, 3)
                pair_products(gp, 0, first=not before)
                if before:
                    project_pairs(gp - 1, (3,))

            def last_slots(gp):
                transpose_rows(gp, 3)
                project_fields(gp, 2)
                gram_rows(gp, 3)
                embed(gp, 2)
                project_pairs(gp - 1, (0,))
                project_fields(gp, 3)
                embed(gp, 3)
                pair_products(gp, 0)
                project_pairs(gp - 1, (1, 2))
                pair_products(gp, 1)
                project_pairs(gp - 1, (3,))
                project_pairs(gp, (0, 1), tail2)
                sum_squares(gp - 1)
                project_pairs(gp, (2, 3), tail2)
                layer1(gp - 1)
                sum_squares(gp, tail2)
                layer1(gp, tail2)
                layer2(gp - 1)
                layer2(gp, tail2, h1_last)
                layer3(gp - 1)
                layer3(gp, tail2, h2_last)

            prepare_embedding()
            prepare_x()
            transpose_rows(0, 0, first=True)
            pe.wait_ge(gram_ready, 1)
            gram_rows(0, 0)
            prepare_b1()
            transpose_rows(0, 1)
            pe.wait_ge(patterns_ready, 1)
            pe.wait_ge(bias_ready, 1)
            pe.wait_ge(x_ready, 1)
            project_fields(0, 0, first=True)
            gram_rows(0, 1)
            pe.wait_ge(wcg_ready, 1)
            embed(0, 0, first=True)
            prepare_xsum()
            prepare_dense(0)
            transpose_rows(0, 2)
            project_fields(0, 1)
            gram_rows(0, 2)
            embed(0, 1)
            prepare_dense(1)
            slots23(0, before=0)
            slots01(1, before=1)
            with pe.Fori(1, NG - 1) as gp:
                slots23(gp)
                slots01(gp + 1)
            last_slots(NG - 1)


def lay_out(inputs):
    import numpy as np
    a = {k: np.asarray(v) for k, v in inputs.items()}
    o = {}
    tables = [a[f"tbl_{f}"] for f in range(NF)]
    start = np.concatenate([[0], np.cumsum([t.shape[0] for t in tables])[:-1]]).astype(np.int32)

    flat = np.arange(TILES * P).reshape(TILES, P)
    bl, fld = flat // NF, flat % NF
    local = (bl // CB) * CHUNK + bl % CB
    b = (np.arange(NG)[:, None, None, None] * GRAN + local.T[None, :, :, None]
         + np.arange(2)[None, None, None, :] * CB)
    n = np.broadcast_to(fld.T[None, :, :, None], b.shape)
    o["ids"] = a["ids"][b, n].transpose(1, 0, 2, 3).reshape(P, -1)
    o["base"] = start[n].transpose(1, 0, 2, 3).reshape(P, -1)
    o["table"] = np.concatenate(tables, axis=0)

    ws = a["L0_rec_Ws"]
    o["ws_t"] = np.concatenate([ws.T, ws.T], axis=0)
    o["gs_row"] = np.broadcast_to(a["L0_rec_gs"], (P, E))
    o["ident"] = np.eye(P, dtype=np.float32)

    row_t = np.array([NPROJ] + list(range(1, NPROJ)))
    quad, r = np.divmod(np.arange(P), 32)
    ti = row_t[r]
    s = 1 + 8 * quad[:, None] + np.arange(KB)[None, :]
    is_x = s == X_SLOT
    tj = np.where(is_x, 0, s)
    gsi, bsi = a["L0_rec_gsi"], a["L0_rec_bsi"]
    sm = np.zeros((P, C_END), np.float32)
    sm[:, C_GD], sm[:, C_BD] = a["L0_rec_gd"], a["L0_rec_bd"]
    sm[:, C_GL:C_GL + LLIVE] = a["L0_rec_gl"][:LIVE].reshape(LLIVE, P).T
    sm[:, C_BL:C_BL + LLIVE] = a["L0_rec_bl"][:LIVE].reshape(LLIVE, P).T
    sm[:, C_B1:C_B1 + OC1] = a["b_top1"].reshape(OC1, P).T
    sm[:, C_B2:C_B2 + OC2] = a["b_top2"].reshape(OC2, P).T
    sm[:, C_W3:C_W3 + OC2] = a["W_top3"].reshape(OC2, P).T
    sm[:, C_GI], sm[:, C_BI] = gsi[ti - 1], bsi[ti - 1]
    sm[:, C_GJ:C_GJ + KB] = np.where(is_x, np.float32(1), gsi[tj - 1])
    sm[:, C_BJ:C_BJ + KB] = np.where(is_x, np.float32(0), bsi[tj - 1])
    sm[:, C_XM:C_XM + KB] = is_x
    o["small"] = sm
    pm = np.zeros((P, KB, 33), np.float32)
    pm[np.arange(P)[:, None], np.arange(KB)[None, :], np.where(is_x, 32, s)] = 1
    dl = np.zeros((P, 32), np.float32)
    dl[np.arange(P), r] = 1
    o["pair_mask"] = np.concatenate([pm.reshape(P, -1), dl], axis=1)

    wsi = a["L0_rec_Wsi"][row_t - 1]
    o["wsi_rows"] = wsi.T[fld.T]
    first = P * np.arange(TILES)[:, None] // NF
    o["span_mask"] = ((bl - first).T[:, :, None] == np.arange(SPAN)).astype(np.float32)
    o["wsi_small"] = wsi.T
    o["bs_rep"] = np.broadcast_to(a["L0_rec_bs"], (NF, E))

    o["wd_t"] = a["L0_rec_Wd"].T.reshape(2, P, E).transpose(1, 0, 2)
    o["dense_t"] = a["r_dense_t"].T.reshape(2, P, B).transpose(1, 0, 2)
    pair = ti[:, None] * (ti[:, None] - 1) // 2 + tj
    wl = np.zeros((P, KB, L), np.float32)
    keep = tj < ti[:, None]
    wl[keep] = a["L0_rec_Wl"].T[pair[keep]]
    o["wl_blocks"] = wl
    w1 = a["W_top1"]
    o["w1_z"] = w1[:LIVE].reshape(LLIVE, P, H1).transpose(1, 0, 2)
    o["w1_d"] = w1[L:].reshape(2, P, H1).transpose(1, 0, 2)
    o["w2"] = a["W_top2"].reshape(OC1, P, H2).transpose(1, 0, 2)
    return {k: np.ascontiguousarray(v) for k, v in o.items()}


def kernel(**inputs):
    import concourse.bacc as _bacc
    from concourse.bass_utils import run_bass_kernel_spmd as _run

    nc = _bacc.Bacc("TRN2", target_bir_lowering=False, num_devices=1)
    arrays, args = {}, {}
    for name, a in lay_out(inputs).items():
        arrays[f"in_{name}_dram"] = a
        args[name] = nc.dram_tensor(f"in_{name}_dram", a.shape, mybir.dt.from_np(a.dtype), kind="ExternalInput").ap()
    out = nc.dram_tensor("out_0_dram", (B, 1), F32, kind="ExternalOutput").ap()
    dlrm_tower(nc, **args, out=out)
    r = _run(nc, [arrays], core_ids=[0])
    return r.results[0]["out_0_dram"]
```

```python
from contextlib import ExitStack

import concourse.bass as bass
from concourse import mybir

F32 = mybir.dt.float32
I32 = mybir.dt.int32
ALU = mybir.AluOpType
ACT = mybir.ActivationFunctionType
AX_X = mybir.AxisListType.X

P = 128
B = 512
NF = 26
D = 64
E = 128
NPROJ = 32
DENSE = 256
L = 512
LIVE = 384
H1, H2 = 512, 256
EPS = 1e-5

GROUP = 64
GRAN = 2 * GROUP
HALF = GRAN // 2
NG = B // GRAN
TILES = GROUP * NF // P
BATCH_END = [4, 7, 10, 13]
NC = len(BATCH_END)
CB = GROUP // NC
CHUNK = 2 * CB
POOL_CHUNKS = (1, 2)
SPAN = 6
SLOTS = NPROJ + 2
X_SLOT, ONE_SLOT = NPROJ, NPROJ + 1
RING = NPROJ // 2
PB = RING * NPROJ // P
PQ = RING // 4
KB = PB + 1
LC, LLIVE = L // P, LIVE // P
OC1, OC2 = H1 // P, H2 // P
ROW_ONE, ROW_X, ROW_XV, ROW_S = 0, 32, 64, 96
C_GD, C_BD, C_GL, C_BL, C_B1 = 0, 1, 2, 2 + LLIVE, 2 + 2 * LLIVE
C_B2 = C_B1 + OC1
C_W3 = C_B2 + OC2
C_GI, C_BI = C_W3 + OC2, C_W3 + OC2 + 1
C_GJ = C_BI + 1
C_BJ = C_GJ + KB
C_END = C_BJ + KB


def batch(c):
    return range(BATCH_END[c - 1] if c else 0, BATCH_END[c])


def tile_spans(j):
    b0, b1 = P * j // NF, (P * j + P - 1) // NF + 1
    out = []
    while b0 < b1:
        end = min(b1, (b0 // CB + 1) * CB)
        out.append((b0 // CB, (b0 % CB) * NPROJ, (b0 - P * j // NF) * NPROJ, (end - b0) * NPROJ))
        b0 = end
    return out


def dlrm_tower(nc, ids_base, table, ws_t, gs_row, ident, small, pair_mask, merge_mask, wsi_rows, span_mask, wsi_small,
               bs_rep, wd_t, dense_t, wl_blocks, w1_z, w1_d, w2, out):
    with ExitStack() as ctx:
        def sb(name, shape, dt=F32):
            return ctx.enter_context(nc.sbuf_tensor(name, shape, dt))

        def sem(name):
            return ctx.enter_context(nc.semaphore(name))

        idx_in = sb("idx_in", [P, 2, NG * 2 * TILES], I32)
        idx = sb("idx", [P, NG * 2 * TILES], I32)
        wc = sb("wc", [P, E])
        wc_nat = sb("wc_nat", [P, P])
        gram = sb("gram", [P, P])
        wcg = sb("wcg", [P, E])
        gs_sb = sb("gs_sb", [P, E])
        eye = sb("eye", [P, P])
        ones = sb("ones", [P, P])
        sm = sb("sm", [P, C_END])
        pmask = sb("pmask", [P, (KB + 1) * NPROJ + KB])
        mmask = sb("mmask", [P, RING], I32)
        wrow = sb("wrow", [P, TILES, NPROJ])
        smask = sb("smask", [P, TILES, SPAN])
        S = sb("S", [P, TILES, SPAN, NPROJ])
        wmean = sb("wmean", [P, TILES])
        wsis = sb("wsis", [NF, NPROJ])
        bsr = sb("bsr", [NF, E])
        tiny = sb("tiny", [P, 16])
        bias_y = sb("bias_y", [P, NPROJ])
        wd = sb("wd", [P, 2, E])
        dns = sb("dns", [P, 2, B])
        wl = sb("wl", [P, KB, L])
        kcoef = sb("kcoef", [P, 4 * KB])
        means = sb("means", [P, KB + 1])
        shift = sb("shift", [P, KB])
        scratch = sb("scratch", [P, KB + 1, L])
        dmat = sb("dmat", [P, KB, P])
        w1z = sb("w1z", [P, LLIVE, H1])
        w1d = sb("w1d", [P, 2, H1])
        w2s = sb("w2s", [P, OC1, H2])
        b1e = sb("b1e", [P, OC1])
        eps = sb("eps", [P, 1])
        warm = sb("warm", [P, 1])
        x_sb = sb("x_sb", [P, B])
        x_sq = sb("x_sq", [P, B])
        x_r = sb("x_r", [P, B])
        h1_dense = sb("h1_dense", [P, OC1, B])
        G = sb("G", [P, TILES, 2, D])
        gt = sb("gt", [P, 4 * P])
        qg = sb("qg", [P, 4 * P])
        var1 = sb("var1", [P, 8])
        sd1 = sb("sd1", [P, 8])
        r1 = sb("r1", [P, 8])
        ut = sb("ut", [P, 512])
        V = sb("V", [P, GRAN, SLOTS])
        sq2 = sb("sq2", [P, CHUNK, NPROJ])
        var2 = sb("var2", [P, CHUNK])
        sd2 = sb("sd2", [P, CHUNK])
        r2 = sb("r2", [P, CHUNK])
        r2_pool = sb("r2_pool", [P, len(POOL_CHUNKS), CHUNK])
        zt = sb("zt", [P, 2, HALF // 4, RING + 2])
        zb = sb("zb", [P, PB, B])
        zx = sb("zx", [P, B])
        f_sb = sb("f_sb", [P, LLIVE, GRAN])
        f_sq = sb("f_sq", [P, LC, GRAN])
        f_sum = sb("f_sum", [P, GRAN])
        sd3 = sb("sd3", [P, GRAN])
        r3 = sb("r3", [P, GRAN])
        zn = sb("zn", [P, LLIVE, GRAN])
        h1_pre = sb("h1_pre", [P, OC1, GRAN])
        h1 = sb("h1", [P, OC1, GRAN])
        h2 = sb("h2", [P, OC2, GRAN])
        h1_last = sb("h1_last", [P, OC1, GRAN])
        h2_last = sb("h2_last", [P, OC2, GRAN])
        y_row = sb("y_row", [1, B])
        ps_gq = ctx.enter_context(nc.psum_tensor("ps_gq", [P, 512], F32))
        ps_tail = ctx.enter_context(nc.psum_tensor("ps_tail", [P, 512], F32))
        ps_ut = ctx.enter_context(nc.psum_tensor("ps_ut", [P, 2, 512], F32))
        ps_y = ctx.enter_context(nc.psum_tensor("ps_y", [P, 2, 512], F32))
        ps_z = ctx.enter_context(nc.psum_tensor("ps_z", [P, 2, 512], F32))
        tail = ps_tail[:, :].rearrange("p (c b) -> p c b", b=GRAN)
        tail2 = ps_y[:, 0, :].rearrange("p (c b) -> p c b", b=GRAN)
        last_h1_ps = ps_ut[:, :, 0:OC1 // 2 * GRAN].rearrange("p h (c b) -> p h c b", b=GRAN)
        last_h2_ps = [ps_gq[:, 0:GRAN], ps_y[:, 1, 0:GRAN]]
        last_y_ps = ps_z[0:1, 0, 0:GRAN]

        ld_ids, ld_wc, ld_ws, ld_wd, ld_pm, ld_sm, ld_s, ld_x, ld_w1z, ld_w1d, ld_w2 = [
            sem(n) for n in ("ld_ids", "ld_wc", "ld_ws", "ld_wd", "ld_pm", "ld_sm", "ld_s", "ld_x", "ld_w1z", "ld_w1d", "ld_w2")]
        ld_wl = [sem("ld_wl_a"), sem("ld_wl_b")]
        gathered = [sem(f"gathered{c}") for c in range(NC)]
        (idx_ready, consts_set, wc_ready, wcg_ready, wc_nat_ps, wc_nat_sb, gram_ps, gram_ready, patterns_ready, wsis_ready,
         bias_ps, bias_ready, wd_ready, xc_ps, x_sq_ready, xvar_ps, x_sd_ready, x_root, x_ready, xsum_ps, xsum_ready,
         b1_ps, b1_ready, dense_ps, dense_ready, w1_ready, last_in_ready, last_ps, last_mean, last_ready, wl_mean, wl_shift, wl_ready) = [
            sem(n) for n in (
                "idx_ready", "consts_set", "wc_ready", "wcg_ready", "wc_nat_ps", "wc_nat_sb", "gram_ps", "gram_ready",
                "patterns_ready", "wsis_ready", "bias_ps", "bias_ready", "wd_ready", "xc_ps", "x_sq_ready", "xvar_ps",
                "x_sd_ready", "x_root", "x_ready", "xsum_ps", "xsum_ready", "b1_ps", "b1_ready", "dense_ps", "dense_ready",
                "w1_ready", "last_in_ready", "last_ps", "last_mean", "last_ready", "wl_mean", "wl_shift", "wl_ready")]
        gt_ps, gt_sb, q_ps, q_used = sem("gt_ps"), sem("gt_sb"), sem("q_ps"), sem("q_used")
        var1_ready, sd1_ready, r1_ready, g_scaled = sem("var1_ready"), sem("sd1_ready"), sem("r1_ready"), sem("g_scaled")
        ut_ps, ut_sb, y_ps, y_sb = sem("ut_ps"), sem("ut_sb"), sem("y_ps"), sem("y_sb")
        sq_ready, var2_ready, sd2_ready, r2_ready, v_ready = (
            sem("sq_ready"), sem("var2_ready"), sem("sd2_ready"), sem("r2_ready"), sem("v_ready"))
        v_pool_ready = sem("v_pool_ready")
        z_ps, z_first, z_merged, z_sb = sem("z_ps"), sem("z_first"), sem("z_merged"), sem("z_sb")
        f_ps, f_sq_ready, f_ready, f_sum_ready, ss_ps = (
            sem("f_ps"), sem("f_sq_ready"), sem("f_ready"), sem("f_sum_ready"), sem("ss_ps"))
        sd3_ready, r3_ready, zn_ready = sem("sd3_ready"), sem("r3_ready"), sem("zn_ready")
        h1_ps, h1_pre_ready, h1_ready, h2_ps, h2_ready = (
            sem("h1_ps"), sem("h1_pre_ready"), sem("h1_ready"), sem("h2_ps"), sem("h2_ready"))
        h1_scaled = sem("h1_scaled")
        yo_ps, yo_ready, stored = sem("yo_ps"), sem("yo_ready"), sem("stored")

        def dense_bank(oc):
            return ps_z[:, oc, :] if oc < 2 else ps_tail[:, :]

        def z_bank():
            return ps_z[:, :, 0:8 * SLOTS].rearrange("p w (b c) -> p w b c", c=SLOTS)

        def chunk_v(c):
            return V[:, c * CHUNK:(c + 1) * CHUNK, 0:NPROJ]

        def nth(gp, c):
            return gp * NC + c + 1

        def half_ocs(h):
            return slice(h * OC1 // 2, (h + 1) * OC1 // 2)

        def nth_half(gp, h):
            return gp * 2 + h + 1


        block = ctx.enter_context(nc.Block())

        @block.sync
        def _(sp):
            sp.dma_start(idx_in[:, :, :], ids_base).then_inc(ld_ids, 16)
            sp.dma_start(wsis[:, :], wsi_small).then_inc(ld_s, 16)
            sp.dma_start(bsr[:, :], bs_rep).then_inc(ld_s, 16)
            sp.dma_start(wrow[:, :, :], wsi_rows).then_inc(ld_s, 16)
            sp.dma_start(smask[:, :, :], span_mask).then_inc(ld_s, 16)
            sp.dma_start(sm[:, :], small).then_inc(ld_sm, 16)
            sp.dma_start(w1z[:, :, :], w1_z).then_inc(ld_w1z, 16)
            sp.wait_ge(gathered[0], 2 * len(batch(0)) * 16)
            sp.dma_start(pmask[:, :], pair_mask).then_inc(ld_pm, 16)
            sp.dma_start(mmask[:, :], merge_mask).then_inc(ld_pm, 16)
            sp.dma_start(w1d[:, :, :], w1_d).then_inc(ld_w1d, 16)
            for h, (k, end) in enumerate(((0, 2), (2, KB))):
                sp.wait_ge(gathered[1 + h], 2 * len(batch(1 + h)) * 16)
                sp.dma_start(wl[:, k:end, :], wl_blocks[:, k:end, :]).then_inc(ld_wl[h], 16)
            sp.wait_ge(gathered[3], 2 * len(batch(3)) * 16)
            sp.dma_start(w2s[:, :, :], w2).then_inc(ld_w2, 16)
            sp.wait_ge(yo_ready, NG)
            sp.dma_start(out.rearrange("b o -> o b"), y_row[:, :]).then_inc(stored, 16)
            sp.wait_ge(stored, 16)

        @block.gpsimd
        def _(pool):
            pool.wait_ge(idx_ready, 1)
            for gp in range(NG):
                for c in range(NC):
                    if gp:
                        pool.wait_ge(ut_ps, nth(gp - 1, c))
                    for j in batch(c):
                        for g in range(2):
                            k = gp * 2 * TILES + 2 * j + g
                            pool.indirect_dma_start(
                                G[:, j, g, :], None, table,
                                bass.IndirectOffsetOnAxis(ap=idx[:, k:k + 1], axis=0)).then_inc(gathered[c], 16)
            for n, c in enumerate(POOL_CHUNKS):
                pool.wait_ge(r2_ready, nth(NG - 1, c))
                pool.tensor_tensor(chunk_v(c), chunk_v(c), r2_pool[:, n, :].unsqueeze(2).broadcast_to([P, CHUNK, NPROJ]),
                                   ALU.mult).then_inc(v_pool_ready, 1)

        @block.scalar
        def _(act):
            act.dma_start(wc[:, :], ws_t).then_inc(ld_wc, 16)
            act.dma_start(wd[:, :, :], wd_t).then_inc(ld_wd, 16)
            act.dma_start(dns[:, :, :], dense_t).then_inc(ld_x, 16)
            act.wait_ge(consts_set, 1)
            act.activation(warm[:, :], eps[:, :], ACT.Sqrt)
            act.dma_start(eye[:, :], ident).then_inc(ld_ws, 16)
            act.dma_start(gs_sb[:, :], gs_row).then_inc(ld_ws, 16)

            def prepare_embedding():
                act.wait_ge(wc_nat_ps, 1)
                act.copy(wc_nat[:, :], ps_ut[:, 0, 0:P]).then_inc(wc_nat_sb, 1)
                act.wait_ge(bias_ps, 1)
                act.copy(bias_y[:, :], ps_y[:, 0, 0:NPROJ]).then_inc(bias_ready, 1)

            def prepare_x():
                act.wait_ge(xc_ps, 1)
                act.activation(x_sq[:, :], ps_y[:, 1, :], ACT.Square).then_inc(x_sq_ready, 1)
                act.wait_ge(xvar_ps, 1)
                act.wait_ge(consts_set, 1)
                act.activation(x_r[:, :], ps_z[:, 0, :], ACT.Sqrt, bias=eps[:, :], scale=1.0 / E).then_inc(x_sd_ready, 1)

            def prepare_w1():
                act.wait_ge(b1_ps, 1)
                for k in range(LLIVE):
                    last = act.activation(w1z[:, k, :], w1z[:, k, :], ACT.Copy, scale=sm[:, C_GL + k:C_GL + k + 1])
                last.then_inc(w1_ready, 1)

            def prepare_dense(oc):
                act.wait_ge(b1_ready, 1)
                act.wait_ge(dense_ps, oc + 1)
                act.activation(h1_dense[:, oc, :], dense_bank(oc), ACT.Identity, bias=b1e[:, oc:oc + 1]).then_inc(dense_ready, 1)

            def prepare_means(h):
                act.wait_ge(ld_wl[h], 16)
                for k in ((0, 1), (2, 3, 4))[h]:
                    last = act.activation(scratch[:, k, :], wl[:, k, :], ACT.Identity, scale=-1.0 / L, accum_out=means[:, k:k + 1])
                last.then_inc(wl_mean, 1)

            def prepare_xsum():
                act.wait_ge(xsum_ps, 1)
                act.copy(zx[ROW_X:ROW_X + 1, :], ps_tail[ROW_X:ROW_X + 1, :]).then_inc(xsum_ready, 1)

            def prepare_last_block():
                act.wait_ge(last_ps, 1)
                act.activation(scratch[:, KB, :], ps_tail[:, :], ACT.Identity, scale=-1.0 / L,
                               accum_out=means[:, KB:KB + 1]).then_inc(last_mean, 1)
                act.wait_ge(last_mean, 1)
                for a, b in ((0, ROW_XV), (ROW_S, P)):
                    last = act.activation(wl[a:b, PB, :], ps_tail[a:b, :], ACT.Identity, bias=means[a:b, KB:KB + 1])
                last.then_inc(last_ready, 1)

            def prepare_gains(blocks):
                act.wait_ge(last_ps, 1)
                act.wait_ge(wl_shift, 1)
                for k in blocks:
                    a, b = (0, P) if k < PB else (ROW_XV, ROW_S)
                    last = act.activation(wl[a:b, k, :], wl[a:b, k, :], ACT.Identity, bias=shift[a:b, k:k + 1],
                                          scale=kcoef[a:b, 3 * KB + k:3 * KB + k + 1])
                last.then_inc(wl_ready, 1)

            def gt_copy(gp, c):
                n = len(batch(c)) * P
                act.wait_ge(gt_ps, nth(gp, c))
                act.copy(gt[:, 0:n], ps_gq[:, 0:n]).then_inc(gt_sb, 1)

            def deviation1(gp, c):
                n = len(batch(c)) * 2
                act.wait_ge(var1_ready, nth(gp, c))
                act.activation(sd1[:, 0:n], var1[:, 0:n], ACT.Sqrt, bias=eps[:, :], scale=1.0 / E).then_inc(sd1_ready, 1)

            def ut_copy(gp, c):
                act.wait_ge(ut_ps, nth(gp, c))
                act.copy(ut[:, :], ps_ut[:, c % 2, :]).then_inc(ut_sb, 1)

            def square2(gp, c):
                act.wait_ge(y_sb, 2 * nth(gp, c))
                act.activation(sq2[:, :, :], chunk_v(c), ACT.Square).then_inc(sq_ready, 1)

            def deviation2(gp, c):
                act.wait_ge(var2_ready, nth(gp, c))
                act.activation(sd2[:, :], var2[:, :], ACT.Sqrt, bias=eps[:, :], scale=1.0 / NPROJ).then_inc(sd2_ready, 1)

            def z_evacuate(gp, h):
                act.wait_ge(z_ps, nth_half(gp, h))
                act.copy(zt[:, h, :, 0:RING].rearrange("p (w b) c -> p w b c", w=2),
                         z_bank()[:, :, :, 0:RING]).then_inc(z_first, 1)

            def z_copy(gp, h, quadrants=range(4)):
                act.wait_ge(z_merged, nth_half(gp, h))
                for qb in quadrants:
                    src = zt[32 * qb:32 * qb + 32, h, :, :].rearrange("p b c -> p c b")
                    at = bass.ds(gp * GRAN + h * HALF + 16 * qb, 16)
                    for q in range(4):
                        act.copy(zb[32 * q:32 * q + 32, :, at], src[:, PQ * q:PQ * q + PQ, :])
                    act.copy(zx[ROW_XV:ROW_XV + 32, at], src[:, RING, :])
                    act.copy(zx[ROW_S:ROW_S + 32, at], src[:, RING + 1, :]).then_inc(z_sb, 1)

            def f_squares(gp, bank=tail):
                act.wait_ge(f_ps, gp + 1)
                act.activation(f_sq[:, :, :], bank, ACT.Square).then_inc(f_sq_ready, 1)

            def f_copy(gp, bank=tail):
                act.copy(f_sb[:, :, :], bank[:, 0:LLIVE, :]).then_inc(f_ready, 1)

            def deviation3(gp, bank=tail):
                act.wait_ge(ss_ps, gp + 1)
                act.activation(sd3[:, :], bank[:, 0, :], ACT.Sqrt, bias=eps[:, :], scale=1.0 / L).then_inc(sd3_ready, 1)

            def relu1(gp):
                act.wait_ge(h1_pre_ready, gp + 1)
                act.activation(h1[:, :, :], h1_pre[:, :, :], ACT.Relu).then_inc(h1_ready, 1)

            def relu2(gp):
                act.wait_ge(h2_ps, gp + 1)
                for oc in range(OC2):
                    last = act.activation(h2[:, oc, :], tail[:, oc, :], ACT.Relu, bias=sm[:, C_B2 + oc:C_B2 + oc + 1])
                last.then_inc(h2_ready, 1)

            def y_copy(gp):
                act.wait_ge(yo_ps, gp + 1)
                act.copy(y_row[:, bass.ds(gp * GRAN, GRAN)], tail[0:1, 0, :]).then_inc(yo_ready, 1)

            def last_relu1(gp, h):
                act.wait_ge(h1_pre_ready, gp + 1 + h)
                act.activation(h1_last[:, half_ocs(h), :], h1_pre[:, half_ocs(h), :], ACT.Relu).then_inc(h1_ready, 1)

            def last_relu2(gp):
                for oc in range(OC2):
                    act.wait_ge(h2_ps, gp + 1 + oc)
                    act.activation(h2_last[:, oc, :], last_h2_ps[oc], ACT.Relu,
                                   bias=sm[:, C_B2 + oc:C_B2 + oc + 1]).then_inc(h2_ready, 1)

            def last_y_copy(gp):
                act.wait_ge(yo_ps, gp + 1)
                act.copy(y_row[:, bass.ds(gp * GRAN, GRAN)], last_y_ps).then_inc(yo_ready, 1)

            def first_slots01(gp):
                gt_copy(gp, 1)
                square2(gp - 1, 3)
                ut_copy(gp, 0)
                z_evacuate(gp - 1, 0)
                deviation2(gp - 1, 3)
                prepare_gains((3, 4))
                deviation1(gp, 1)
                z_copy(gp - 1, 0, (0, 1))

                gt_copy(gp, 2)
                square2(gp, 0)
                ut_copy(gp, 1)
                z_evacuate(gp - 1, 1)
                prepare_dense(2)
                deviation1(gp, 2)
                deviation2(gp, 0)
                z_copy(gp - 1, 1, (0, 1))
                prepare_dense(3)

            def slots01(gp):
                gt_copy(gp, 1)
                f_squares(gp - 2)
                deviation2(gp - 1, 3)
                ut_copy(gp, 0)
                f_copy(gp - 2)
                deviation3(gp - 2)
                deviation1(gp, 1)
                z_copy(gp - 1, 0)
                square2(gp, 0)
                z_evacuate(gp - 1, 1)

                gt_copy(gp, 2)
                relu1(gp - 2)
                ut_copy(gp, 1)
                deviation2(gp, 0)
                z_copy(gp - 1, 1, (0, 1))
                deviation1(gp, 2)
                relu2(gp - 2)
                z_copy(gp - 1, 1, (2, 3))
                y_copy(gp - 2)

            def slots23(gp, first=False):
                gt_copy(gp, 3)
                ut_copy(gp, 2)
                square2(gp, 1)
                deviation1(gp, 3)
                deviation2(gp, 1)
                if first:
                    prepare_means(1)
                square2(gp, 2)

                gt_copy(gp + 1, 0)
                ut_copy(gp, 3)
                deviation2(gp, 2)
                if first:
                    prepare_last_block()
                deviation1(gp + 1, 0)
                if not first:
                    square2(gp, 3)
                    z_evacuate(gp, 0)
                else:
                    prepare_gains((0, 1, 2))

            def last_slots(gp):
                gt_copy(gp, 3)
                ut_copy(gp, 2)
                square2(gp, 1)
                deviation1(gp, 3)
                deviation2(gp, 1)
                ut_copy(gp, 3)
                square2(gp, 2)
                deviation2(gp, 2)
                square2(gp, 3)
                f_squares(gp - 1)
                f_copy(gp - 1)
                deviation2(gp, 3)
                z_evacuate(gp, 0)
                deviation3(gp - 1)
                z_copy(gp, 0, (0, 1))
                z_evacuate(gp, 1)
                z_copy(gp, 1, (0, 1))
                relu1(gp - 1)
                act.wait_ge(zn_ready, gp)
                act.wait_ge(f_ps, gp + 1)
                f_copy(gp, tail2)
                f_squares(gp, tail2)
                deviation3(gp, tail2)
                last_relu1(gp, 0)
                last_relu1(gp, 1)
                relu2(gp - 1)
                last_relu2(gp)
                y_copy(gp - 1)
                last_y_copy(gp)

            prepare_embedding()
            prepare_x()
            gt_copy(0, 0)
            deviation1(0, 0)
            prepare_w1()
            gt_copy(0, 1)
            ut_copy(0, 0)
            deviation1(0, 1)
            square2(0, 0)
            gt_copy(0, 2)
            ut_copy(0, 1)
            prepare_xsum()
            prepare_dense(0)
            deviation2(0, 0)
            deviation1(0, 2)
            prepare_means(0)
            prepare_dense(1)
            slots23(0, first=True)
            first_slots01(1)
            with act.Fori(1, NG - 1) as gp:
                slots23(gp)
                slots01(gp + 1)
            last_slots(NG - 1)

        @block.vector
        def _(dve):
            chain = sem("dve_chain")
            count = [0]

            def link(ins):
                count[0] += 1
                ins.then_inc(chain, 1)
                dve.wait_ge(chain, count[0])

            def prepare_embedding():
                dve.wait_ge(ld_ids, 16)
                dve.tensor_tensor(idx[:, :], idx_in[:, 0, :], idx_in[:, 1, :], ALU.add).then_inc(idx_ready, 1)
                dve.wait_ge(ld_wc, 16)
                link(dve.reduce_sum(tiny[:, 0:1], wc[:, :], AX_X))
                link(dve.tensor_scalar(tiny[:, 0:1], tiny[:, 0:1], -1.0 / E, None, ALU.mult))
                dve.tensor_scalar(wc[:, :], wc[:, :], tiny[:, 0:1], None, ALU.add).then_inc(wc_ready, 1)

            def prepare_gram():
                dve.wait_ge(gram_ps, 1)
                for h in (0, 64):
                    last = dve.tensor_copy(gram[h:h + 64, h:h + 64], ps_ut[h:h + 64, 1, h:h + 64])
                last.then_inc(gram_ready, 1)
                dve.wait_ge(ld_ws, 32)
                dve.tensor_tensor(wcg[:, :], wc[:, :], gs_sb[:, :], ALU.mult).then_inc(wcg_ready, 1)

            def prepare_wsis():
                dve.wait_ge(ld_s, 64)
                link(dve.reduce_sum(tiny[0:NF, 1:2], wsis[:, :], AX_X))
                link(dve.tensor_scalar(tiny[0:NF, 1:2], tiny[0:NF, 1:2], -1.0 / NPROJ, None, ALU.mult))
                dve.tensor_scalar(wsis[:, :], wsis[:, :], tiny[0:NF, 1:2], None, ALU.add).then_inc(wsis_ready, 1)

            def prepare_wd():
                dve.wait_ge(ld_wd, 16)
                link(dve.reduce_sum(tiny[:, 2:4], wd[:, :, :], AX_X))
                link(dve.tensor_scalar(tiny[:, 2:4], tiny[:, 2:4], -1.0 / E, None, ALU.mult))
                for k in range(2):
                    last = dve.tensor_scalar(wd[:, k, :], wd[:, k, :], tiny[:, 2 + k:3 + k], None, ALU.add)
                last.then_inc(wd_ready, 1)

            def prepare_constants():
                dve.memset(eps[:, :], EPS).then_inc(consts_set, 1)
                dve.memset(gram[:, :], 0.0)
                dve.memset(ones[:, :], 1.0)
                dve.memset(dmat[:, :, :], 0.0)
                dve.memset(V[:, :, ONE_SLOT], 1.0)
                link(dve.memset(zx[:, :], 0.0))
                dve.memset(zx[ROW_ONE:ROW_ONE + 1, :], 1.0).then_inc(consts_set, 1)

            def prepare_patterns():
                link(dve.reduce_sum(wmean[:, :], wrow[:, :, :], AX_X))
                link(dve.tensor_scalar(wmean[:, :], wmean[:, :], -1.0 / NPROJ, None, ALU.mult))
                link(dve.tensor_tensor(wrow[:, :, :], wrow[:, :, :],
                                       wmean[:, :].unsqueeze(2).broadcast_to([P, TILES, NPROJ]), ALU.add))
                dve.tensor_tensor(S[:, :, :, :], wrow[:, :, :].unsqueeze(2).broadcast_to([P, TILES, SPAN, NPROJ]),
                                  smask[:, :, :].unsqueeze(3).broadcast_to([P, TILES, SPAN, NPROJ]),
                                  ALU.mult).then_inc(patterns_ready, 1)

            def prepare_b1():
                dve.wait_ge(ld_sm, 16)
                dve.wait_ge(b1_ps, 1)
                dve.tensor_tensor(b1e[:, :], ps_tail[:, 0:OC1], sm[:, C_B1:C_B1 + OC1], ALU.add).then_inc(b1_ready, 1)

            def prepare_x_root(h):
                if h == 0:
                    dve.wait_ge(x_sd_ready, 1)
                dve.reciprocal(x_sq[:, h * B // 2:(h + 1) * B // 2], x_r[:, h * B // 2:(h + 1) * B // 2]).then_inc(x_root, 1)

            def prepare_x():
                dve.wait_ge(ld_sm, 16)
                dve.wait_ge(x_root, 2)
                link(dve.tensor_tensor(x_sb[:, :], ps_y[:, 1, :], x_sq[:, :], ALU.mult))
                dve.tensor_scalar(x_sb[:, :], x_sb[:, :], sm[:, C_GD:C_GD + 1], sm[:, C_BD:C_BD + 1],
                                  ALU.mult, ALU.add).then_inc(x_ready, 1)

            def prepare_last_block():
                dve.wait_ge(ld_pm, 32)
                gj, bj = (sm[:, c:c + KB] for c in (C_GJ, C_BJ))
                gi, bi = sm[:, C_GI:C_GI + 1], sm[:, C_BI:C_BI + 1]
                k_gb, k_bg, k_bb, k_gg = (kcoef[:, n * KB:(n + 1) * KB] for n in range(4))
                dve.tensor_scalar(k_gb, bj, gi, None, ALU.mult)
                dve.tensor_scalar(k_bg, gj, bi, None, ALU.mult)
                dve.tensor_scalar(k_bb, bj, bi, float(E), ALU.mult, ALU.mult)
                link(dve.tensor_scalar(k_gg, gj, gi, None, ALU.mult))
                second = pmask[:, 0:KB * NPROJ].rearrange("p (k c) -> p k c", c=NPROJ)
                first = pmask[:, KB * NPROJ:(KB + 1) * NPROJ]
                with_x = pmask[:, (KB + 1) * NPROJ:]
                dve.tensor_tensor(dmat[:, :, ROW_X], with_x, k_bg, ALU.mult)
                dve.tensor_copy(dmat[:, :, ROW_ONE], k_bb)
                link(dve.tensor_tensor(dmat[:, :, ROW_S:ROW_S + 32], second,
                                       k_bg.unsqueeze(2).broadcast_to([P, KB, NPROJ]), ALU.mult))
                for k in range(KB):
                    last = dve.scalar_tensor_tensor(dmat[:, k, ROW_S:ROW_S + 32], first, k_gb[:, k:k + 1],
                                                    dmat[:, k, ROW_S:ROW_S + 32], ALU.mult, ALU.add)
                last.then_inc(last_in_ready, 1)

            def prepare_shift():
                dve.wait_ge(wl_mean, 2)
                dve.tensor_tensor(shift[:, :], means[:, 0:KB], kcoef[:, 3 * KB:4 * KB], ALU.mult).then_inc(wl_shift, 1)

            def variance1(gp, c):
                js = batch(c)
                n = len(js)
                dve.wait_ge(q_ps, nth(gp, c))
                dve.tensor_tensor(qg[:, 0:n * P], ps_gq[:, 0:n * P],
                                  G[:, js[0]:js[0] + n, :, :].rearrange("p j g d -> p (j g d)"),
                                  ALU.mult).then_inc(q_used, 1)
                dve.wait_ge(q_used, nth(gp, c))
                dve.reduce_sum(var1[:, 0:2 * n], qg[:, 0:n * P].rearrange("p (t d) -> p t d", d=D), AX_X).then_inc(var1_ready, 1)

            def scale_rows(gp, c):
                js = batch(c)
                n = 2 * len(js)
                dve.wait_ge(sd1_ready, nth(gp, c))
                dve.reciprocal(r1[:, 0:n], sd1[:, 0:n]).then_inc(r1_ready, 1)
                dve.wait_ge(r1_ready, nth(gp, c))
                rows = G[:, js[0]:js[0] + n // 2, :, :].rearrange("p j g d -> p (j g) d")
                dve.tensor_tensor(rows, rows, r1[:, 0:n].unsqueeze(2).broadcast_to([P, n, D]), ALU.mult).then_inc(g_scaled, 1)

            def x_slots(gp, h):
                dve.tensor_copy(V[:, h * HALF:(h + 1) * HALF, X_SLOT], x_sb[:, bass.ds(gp * GRAN + h * HALF, HALF)])

            def y_evacuate(gp, c):
                for g in range(2):
                    dve.wait_ge(y_ps, 2 * nth(gp, c) - 1 + g)
                    b0 = c * CHUNK + g * CB
                    dve.tensor_tensor(V[:, b0:b0 + CB, 0:NPROJ], ps_y[:, g, :].rearrange("p (b q) -> p b q", q=NPROJ),
                                      bias_y[:, :].unsqueeze(1).broadcast_to([P, CB, NPROJ]), ALU.add).then_inc(y_sb, 1)

            def variance2(gp, c):
                dve.wait_ge(sq_ready, nth(gp, c))
                dve.reduce_sum(var2[:, :], sq2[:, :, :], AX_X).then_inc(var2_ready, 1)

            def normalise2(gp, c):
                dve.wait_ge(sd2_ready, nth(gp, c))
                dve.reciprocal(r2[:, :], sd2[:, :]).then_inc(r2_ready, 1)
                dve.wait_ge(r2_ready, nth(gp, c))
                dve.tensor_tensor(chunk_v(c), chunk_v(c), r2[:, :].unsqueeze(2).broadcast_to([P, CHUNK, NPROJ]),
                                  ALU.mult).then_inc(v_ready, 1)

            def sum_blocks3(gp):
                dve.wait_ge(f_sq_ready, gp + 1)
                dve.reduce_sum(f_sum[:, :], f_sq[:, :, :].rearrange("p c b -> p b c"), AX_X).then_inc(f_sum_ready, 1)

            def normalise3(gp):
                dve.wait_ge(sd3_ready, gp + 1)
                dve.reciprocal(r3[:, :], sd3[:, :]).then_inc(r3_ready, 1)
                dve.wait_ge(r3_ready, gp + 1)
                dve.tensor_tensor(zn[:, :, :], f_sb[:, :, :], r3[:, :].unsqueeze(1).broadcast_to([P, LLIVE, GRAN]),
                                  ALU.mult).then_inc(zn_ready, 1)

            def add_dense(gp):
                dve.wait_ge(h1_ps, gp + 1)
                dve.tensor_tensor(h1_pre[:, :, :], tail, h1_dense[:, :, bass.ds(gp * GRAN, GRAN)],
                                  ALU.add).then_inc(h1_pre_ready, 1)

            def last_normalise3(gp):
                dve.wait_ge(sd3_ready, gp + 1)
                dve.reciprocal(r3[:, :], sd3[:, :]).then_inc(r3_ready, 1)
                dve.wait_ge(r3_ready, gp + 1)
                dve.wait_ge(h1_ready, gp)
                for h in range(2):
                    dve.wait_ge(h1_ps, gp + 1 + h)
                    dve.tensor_tensor(h1_pre[:, half_ocs(h), :], last_h1_ps[:, h, :, :],
                                      r3[:, :].unsqueeze(1).broadcast_to([P, OC1 // 2, GRAN]),
                                      ALU.mult).then_inc(h1_scaled, 1)
                    dve.wait_ge(h1_scaled, h + 1)
                    dve.tensor_tensor(h1_pre[:, half_ocs(h), :], h1_pre[:, half_ocs(h), :],
                                      h1_dense[:, half_ocs(h), bass.ds(gp * GRAN, GRAN)],
                                      ALU.add).then_inc(h1_pre_ready, 1)

            def z_merge(gp, h):
                dve.wait_ge(z_first, nth_half(gp, h))
                dst = zt[:, h, :, :].rearrange("p (w b) c -> p w b c", w=2)
                dve.tensor_copy(dst[:, :, :, RING:RING + 2], z_bank()[:, :, :, NPROJ:SLOTS])
                dve.copy_predicated(dst[:, :, :, 0:RING],
                                    mmask[:, :].unsqueeze(1).unsqueeze(1).broadcast_to([P, 2, 8, RING]),
                                    z_bank()[:, :, :, RING:NPROJ]).then_inc(z_merged, 1)

            def z_copy(gp, h, quadrants=range(4)):
                dve.wait_ge(z_merged, nth_half(gp, h))
                for qb in quadrants:
                    src = zt[32 * qb:32 * qb + 32, h, :, :].rearrange("p b c -> p c b")
                    at = bass.ds(gp * GRAN + h * HALF + 16 * qb, 16)
                    for q in range(4):
                        dve.tensor_copy(zb[32 * q:32 * q + 32, :, at], src[:, PQ * q:PQ * q + PQ, :])
                    dve.tensor_copy(zx[ROW_XV:ROW_XV + 32, at], src[:, RING, :])
                    dve.tensor_copy(zx[ROW_S:ROW_S + 32, at], src[:, RING + 1, :]).then_inc(z_sb, 1)

            def first_slots01(gp):
                z_merge(gp - 1, 0)
                normalise2(gp - 1, 3)
                variance1(gp, 1)
                scale_rows(gp, 1)
                dve.wait_ge(z_ps, nth_half(gp - 1, 0))
                x_slots(gp, 0)
                y_evacuate(gp, 0)
                z_copy(gp - 1, 0, (2, 3))

                variance1(gp, 2)
                variance2(gp, 0)
                scale_rows(gp, 2)
                z_merge(gp - 1, 1)
                normalise2(gp, 0)
                y_evacuate(gp, 1)
                z_copy(gp - 1, 1, (2, 3))

            def slots01(gp):
                z_merge(gp - 1, 0)
                sum_blocks3(gp - 2)
                normalise2(gp - 1, 3)
                variance1(gp, 1)
                normalise3(gp - 2)
                scale_rows(gp, 1)
                dve.wait_ge(z_ps, nth_half(gp - 1, 0))
                x_slots(gp, 0)
                y_evacuate(gp, 0)

                add_dense(gp - 2)
                variance2(gp, 0)
                z_merge(gp - 1, 1)
                variance1(gp, 2)
                normalise2(gp, 0)
                scale_rows(gp, 2)
                y_evacuate(gp, 1)

            def slots23(gp, first=False):
                variance1(gp, 3)
                variance2(gp, 1)
                scale_rows(gp, 3)
                if not first:
                    dve.wait_ge(z_ps, nth_half(gp - 1, 1))
                x_slots(gp, 1)
                y_evacuate(gp, 2)
                normalise2(gp, 1)
                variance2(gp, 2)

                if first:
                    prepare_shift()
                variance1(gp + 1, 0)
                normalise2(gp, 2)
                if first:
                    scale_rows(gp + 1, 0)
                y_evacuate(gp, 3)
                if not first:
                    scale_rows(gp + 1, 0)
                variance2(gp, 3)

            def root2(gp, c):
                dve.wait_ge(sd2_ready, nth(gp, c))
                dve.reciprocal(r2_pool[:, POOL_CHUNKS.index(c), :], sd2[:, :]).then_inc(r2_ready, 1)

            def last_slots(gp):
                variance1(gp, 3)
                variance2(gp, 1)
                scale_rows(gp, 3)
                dve.wait_ge(z_ps, nth_half(gp - 1, 1))
                x_slots(gp, 1)
                y_evacuate(gp, 2)
                root2(gp, 1)
                variance2(gp, 2)
                y_evacuate(gp, 3)
                root2(gp, 2)
                variance2(gp, 3)
                normalise2(gp, 3)
                z_merge(gp, 0)
                normalise3(gp - 1)
                z_copy(gp, 0, (2, 3))
                z_merge(gp, 1)
                z_copy(gp, 1, (2, 3))
                add_dense(gp - 1)
                last_normalise3(gp)

            prepare_constants()
            prepare_embedding()
            prepare_wd()
            prepare_wsis()
            prepare_gram()
            prepare_patterns()
            prepare_x_root(0)
            variance1(0, 0)
            scale_rows(0, 0)
            prepare_x_root(1)
            prepare_x()
            prepare_b1()
            variance1(0, 1)
            scale_rows(0, 1)
            x_slots(0, 0)
            dve.wait_ge(bias_ready, 1)
            y_evacuate(0, 0)
            variance2(0, 0)
            variance1(0, 2)
            normalise2(0, 0)
            scale_rows(0, 2)
            y_evacuate(0, 1)
            prepare_last_block()
            slots23(0, first=True)
            first_slots01(1)
            with dve.Fori(1, NG - 1) as gp:
                slots23(gp)
                slots01(gp + 1)
            last_slots(NG - 1)

        @block.tensor
        def _(pe):
            def prepare_embedding():
                pe.wait_ge(ld_ws, 32)
                pe.wait_ge(wc_ready, 1)
                pe.transpose(ps_ut[:, 0, 0:P], wc[:, :], eye[:, :]).then_inc(wc_nat_ps, 1)
                pe.wait_ge(wc_nat_sb, 1)
                pe.matmul(ps_ut[:, 1, 0:P], wc_nat[:, :], wc_nat[:, :], start=True, stop=True).then_inc(gram_ps, 1)
                pe.wait_ge(wsis_ready, 1)
                pe.wait_ge(ld_s, 64)
                pe.matmul(ps_y[:, 0, 0:NPROJ], bsr[:, :], wsis[:, :], start=True, stop=True).then_inc(bias_ps, 1)

            def prepare_x():
                pe.wait_ge(wd_ready, 1)
                pe.wait_ge(ld_x, 16)
                for k in range(2):
                    mm = pe.matmul(ps_y[:, 1, :], wd[:, k, :], dns[:, k, :], start=(k == 0), stop=(k == 1))
                mm.then_inc(xc_ps, 1)
                pe.wait_ge(x_sq_ready, 1)
                pe.wait_ge(consts_set, 2)
                pe.matmul(ps_z[:, 0, :], ones[:, :], x_sq[:, :], start=True, stop=True).then_inc(xvar_ps, 1)

            def prepare_b1():
                pe.wait_ge(ld_w1z, 16)
                pe.wait_ge(ld_sm, 16)
                for oc in range(OC1):
                    for k in range(LLIVE):
                        mm = pe.matmul(ps_tail[:, oc:oc + 1], w1z[:, k, oc * P:(oc + 1) * P],
                                       sm[:, C_BL + k:C_BL + k + 1], start=(k == 0), stop=(k == LLIVE - 1))
                mm.then_inc(b1_ps, 1)

            def prepare_dense(oc):
                pe.wait_ge(ld_w1d, 16)
                if oc == 0:
                    pe.wait_ge(x_sd_ready, 1)
                if oc == 2:
                    pe.wait_ge(last_ready, 1)
                if oc == 3:
                    pe.wait_ge(dense_ready, 3)
                for k in range(2):
                    mm = pe.matmul(dense_bank(oc), w1d[:, k, oc * P:(oc + 1) * P], dns[:, k, :],
                                   start=(k == 0), stop=(k == 1))
                mm.then_inc(dense_ps, 1)

            def prepare_xsum():
                pe.wait_ge(b1_ready, 1)
                pe.matmul(ps_tail[ROW_X:ROW_X + 1, :], ones[:, 0:1], x_sb[:, :], start=True, stop=True).then_inc(xsum_ps, 1)

            def prepare_last_block():
                for loaded in ld_wl:
                    pe.wait_ge(loaded, 16)
                pe.wait_ge(last_in_ready, 1)
                pe.wait_ge(xsum_ready, 1)
                for k in range(KB):
                    mm = pe.matmul(ps_tail[:, :], dmat[:, k, :], wl[:, k, :], start=(k == 0), stop=(k == KB - 1))
                mm.then_inc(last_ps, 1)

            def transpose_rows(gp, c, first=False):
                js = batch(c)
                pe.wait_ge(gathered[c], (gp + 1) * 2 * len(js) * 16)
                if not first:
                    pe.wait_ge(q_used, nth(gp, c) - 1)
                for n, j in enumerate(js):
                    mm = pe.transpose(ps_gq[:, n * P:(n + 1) * P], G[:, j, :, :].rearrange("p g d -> p (g d)"), eye[:, :])
                mm.then_inc(gt_ps, 1)

            def gram_rows(gp, c):
                pe.wait_ge(gt_sb, nth(gp, c))
                for n in range(len(batch(c))):
                    mm = pe.matmul(ps_gq[:, n * P:(n + 1) * P], gt[:, n * P:(n + 1) * P], gram[:, :], start=True, stop=True)
                mm.then_inc(q_ps, 1)

            def project_fields(gp, c, first=False):
                pe.wait_ge(g_scaled, nth(gp, c))
                if not first:
                    pe.wait_ge(ut_sb, nth(gp, c) - 1)
                for j in batch(c):
                    for chunk, col, scol, n in tile_spans(j):
                        begins = (P * j // NF) // CB != chunk or (P * j) % (CB * NF) == 0
                        mm = pe.matmul(ps_ut[:, chunk % 2, col:col + n], G[:, j, :, :].rearrange("p g d -> p (g d)"),
                                       S[:, j, :, :].rearrange("p s q -> p (s q)")[:, scol:scol + n],
                                       start=begins, stop=True, skip_group_check=True)
                mm.then_inc(ut_ps, 1)

            def embed(gp, c, first=False):
                pe.wait_ge(ut_sb, nth(gp, c))
                for g in range(2):
                    if not first:
                        pe.wait_ge(y_sb, 2 * nth(gp, c) - 3 + g)
                    pe.matmul(ps_y[:, g, :], wcg[64 * g:64 * g + 64, :], ut[64 * g:64 * g + 64, :],
                              start=True, stop=True).then_inc(y_ps, 1)

            def pair_products(gp, h, first=False, last=False):
                if last:
                    pe.wait_ge(v_ready, nth(gp, 0) + h)
                    pe.wait_ge(v_pool_ready, h + 1)
                else:
                    pe.wait_ge(v_ready, nth(gp, 2 * h + 1))
                if first:
                    pe.wait_ge(dense_ready, 2)
                else:
                    pe.wait_ge(z_merged, nth_half(gp, h) - 1)
                for bb in range(16):
                    for qb in range(4):
                        b = h * HALF + 16 * qb + bb
                        col = (bb % 8) * SLOTS
                        mm = pe.matmul(ps_z[32 * qb:32 * qb + 32, bb // 8, col:col + SLOTS], V[:, b, 0:NPROJ],
                                       V[:, b, :], start=True, stop=True)
                mm.then_inc(z_ps, 1)

            def project_pairs(gp, lcs, bank=tail):
                if lcs[0] == 0:
                    pe.wait_ge(wl_ready, 2)
                    pe.wait_ge(dense_ready, OC1)
                    pe.wait_ge(z_sb, 4 * nth_half(gp, 1))
                for lc in lcs:
                    for k in range(KB):
                        rhs = (zb[:, k, :] if k < PB else zx[:, :])[:, bass.ds(gp * GRAN, GRAN)]
                        mm = pe.matmul(bank[:, lc, :], wl[:, k, lc * P:(lc + 1) * P], rhs, start=(k == 0), stop=(k == KB - 1))
                if lcs[-1] == LC - 1:
                    mm.then_inc(f_ps, 1)

            def sum_squares(gp, bank=tail):
                pe.wait_ge(f_sum_ready, gp + 1)
                pe.wait_ge(f_ready, gp + 1)
                pe.matmul(bank[:, 0, :], ones[:, :], f_sum[:, :], start=True, stop=True).then_inc(ss_ps, 1)

            def sum_all_squares(gp, bank=tail):
                pe.wait_ge(f_sq_ready, gp + 1)
                pe.wait_ge(f_ready, gp + 1)
                for lc in range(LC):
                    mm = pe.matmul(bank[:, 0, :], ones[:, :], f_sq[:, lc, :], start=(lc == 0), stop=(lc == LC - 1))
                mm.then_inc(ss_ps, 1)

            def layer1(gp):
                pe.wait_ge(w1_ready, 1)
                pe.wait_ge(zn_ready, gp + 1)
                for oc in range(OC1):
                    for k in range(LLIVE):
                        mm = pe.matmul(tail[:, oc, :], w1z[:, k, oc * P:(oc + 1) * P], zn[:, k, :],
                                       start=(k == 0), stop=(k == LLIVE - 1))
                mm.then_inc(h1_ps, 1)

            def layer2(gp, ocs=range(OC2)):
                pe.wait_ge(ld_w2, 16)
                pe.wait_ge(h1_ready, gp + 1)
                for oc in ocs:
                    for k in range(OC1):
                        mm = pe.matmul(tail[:, oc, :], w2s[:, k, oc * P:(oc + 1) * P], h1[:, k, :],
                                       start=(k == 0), stop=(k == OC1 - 1))
                if OC2 - 1 in ocs:
                    mm.then_inc(h2_ps, 1)

            def layer3(gp):
                pe.wait_ge(h2_ready, gp + 1)
                for k in range(OC2):
                    mm = pe.matmul(tail[0:1, 0, :], sm[:, C_W3 + k:C_W3 + k + 1], h2[:, k, :],
                                   start=(k == 0), stop=(k == OC2 - 1))
                mm.then_inc(yo_ps, 1)

            def last_layer1(gp, ocs):
                pe.wait_ge(f_ready, gp + 1)
                for oc in ocs:
                    h = oc * 2 // OC1
                    for k in range(LLIVE):
                        mm = pe.matmul(last_h1_ps[:, h, oc % (OC1 // 2), :], w1z[:, k, oc * P:(oc + 1) * P], f_sb[:, k, :],
                                       start=(k == 0), stop=(k == LLIVE - 1))
                    if (oc + 1) % (OC1 // 2) == 0:
                        mm.then_inc(h1_ps, 1)

            def last_layer2(gp):
                for h in range(2):
                    pe.wait_ge(h1_ready, gp + 1 + h)
                    for oc in range(OC2):
                        for k in range(h * OC1 // 2, (h + 1) * OC1 // 2):
                            mm = pe.matmul(last_h2_ps[oc], w2s[:, k, oc * P:(oc + 1) * P], h1_last[:, k, :],
                                           start=(k == 0), stop=(k == OC1 - 1))
                        if h == 1:
                            mm.then_inc(h2_ps, 1)

            def last_layer3(gp):
                for k in range(OC2):
                    pe.wait_ge(h2_ready, gp + 1 + k)
                    mm = pe.matmul(last_y_ps, sm[:, C_W3 + k:C_W3 + k + 1], h2_last[:, k, :],
                                   start=(k == 0), stop=(k == OC2 - 1))
                mm.then_inc(yo_ps, 1)

            def first_slots01(gp):
                transpose_rows(gp, 1)
                project_fields(gp, 0)
                gram_rows(gp, 1)
                embed(gp, 0)
                prepare_dense(2)
                pair_products(gp - 1, 1)

                transpose_rows(gp, 2)
                project_fields(gp, 1)
                gram_rows(gp, 2)
                embed(gp, 1)
                prepare_dense(3)

            def slots01(gp):
                transpose_rows(gp, 1)
                project_fields(gp, 0)
                gram_rows(gp, 1)
                embed(gp, 0)
                sum_squares(gp - 2)
                pair_products(gp - 1, 1)
                layer1(gp - 2)

                transpose_rows(gp, 2)
                project_fields(gp, 1)
                gram_rows(gp, 2)
                layer2(gp - 2)
                embed(gp, 1)
                layer3(gp - 2)

            def slots23(gp, first=False):
                transpose_rows(gp, 3)
                project_fields(gp, 2)
                gram_rows(gp, 3)
                embed(gp, 2)
                if not first:
                    project_pairs(gp - 1, (0, 1, 2))
                else:
                    prepare_last_block()

                transpose_rows(gp + 1, 0)
                project_fields(gp, 3)
                gram_rows(gp + 1, 0)
                embed(gp, 3)
                pair_products(gp, 0, first)
                if not first:
                    project_pairs(gp - 1, (3,))

            def last_slots(gp):
                transpose_rows(gp, 3)
                project_fields(gp, 2)
                gram_rows(gp, 3)
                embed(gp, 2)
                project_pairs(gp - 1, (0,))
                project_fields(gp, 3)
                project_pairs(gp - 1, (1,))
                embed(gp, 3)
                project_pairs(gp - 1, (2, 3))
                pair_products(gp, 0, last=True)
                sum_all_squares(gp - 1)
                pair_products(gp, 1, last=True)
                layer1(gp - 1)
                project_pairs(gp, range(LC), tail2)
                layer2(gp - 1, ocs=range(1))
                last_layer1(gp, range(1))
                sum_all_squares(gp, tail2)
                last_layer1(gp, range(1, OC1))
                layer2(gp - 1, ocs=range(1, OC2))
                last_layer2(gp)
                layer3(gp - 1)
                last_layer3(gp)

            prepare_embedding()
            prepare_x()
            transpose_rows(0, 0, first=True)
            pe.wait_ge(gram_ready, 1)
            gram_rows(0, 0)
            prepare_b1()
            transpose_rows(0, 1)
            pe.wait_ge(patterns_ready, 1)
            project_fields(0, 0, first=True)
            gram_rows(0, 1)
            pe.wait_ge(bias_ready, 1)
            pe.wait_ge(x_ready, 1)
            pe.wait_ge(wcg_ready, 1)
            embed(0, 0, first=True)
            prepare_xsum()
            prepare_dense(0)
            transpose_rows(0, 2)
            project_fields(0, 1)
            gram_rows(0, 2)
            embed(0, 1)
            prepare_dense(1)
            slots23(0, first=True)
            first_slots01(1)
            with pe.Fori(1, NG - 1) as gp:
                slots23(gp)
                slots01(gp + 1)
            last_slots(NG - 1)


def lay_out(inputs):
    import numpy as np
    a = {k: np.asarray(v) for k, v in inputs.items()}
    o = {}
    tables = [a[f"tbl_{f}"] for f in range(NF)]
    start = np.concatenate([[0], np.cumsum([t.shape[0] for t in tables])[:-1]]).astype(np.int32)

    flat = np.arange(TILES * P).reshape(TILES, P)
    bl, fld = flat // NF, flat % NF
    local = (bl // CB) * CHUNK + bl % CB
    b = (np.arange(NG)[:, None, None, None] * GRAN + local.T[None, :, :, None]
         + np.arange(2)[None, None, None, :] * CB)
    n = np.broadcast_to(fld.T[None, :, :, None], b.shape)
    o["ids_base"] = np.stack([v.transpose(1, 0, 2, 3).reshape(P, -1) for v in (a["ids"][b, n], start[n])], axis=1)
    o["table"] = np.concatenate(tables, axis=0)

    ws = a["L0_rec_Ws"]
    o["ws_t"] = np.concatenate([ws.T, ws.T], axis=0)
    o["gs_row"] = np.broadcast_to(a["L0_rec_gs"], (P, E))
    o["ident"] = np.eye(P, dtype=np.float32)

    row_t = np.array([NPROJ] + list(range(1, NPROJ)))
    quad, r = np.divmod(np.arange(P), 32)
    m = PQ * quad[:, None] + np.arange(PB)[None, :]
    second = (r[:, None] - m) % NPROJ > RING
    s = np.where(second, m + RING, m)
    gsi, bsi = a["L0_rec_gsi"], a["L0_rec_bsi"]
    ti, tj = row_t[r], row_t[s]
    sm = np.zeros((P, C_END), np.float32)
    sm[:, C_GD], sm[:, C_BD] = a["L0_rec_gd"], a["L0_rec_bd"]
    sm[:, C_GL:C_GL + LLIVE] = a["L0_rec_gl"][:LIVE].reshape(LLIVE, P).T
    sm[:, C_BL:C_BL + LLIVE] = a["L0_rec_bl"][:LIVE].reshape(LLIVE, P).T
    sm[:, C_B1:C_B1 + OC1] = a["b_top1"].reshape(OC1, P).T
    sm[:, C_B2:C_B2 + OC2] = a["b_top2"].reshape(OC2, P).T
    sm[:, C_W3:C_W3 + OC2] = a["W_top3"].reshape(OC2, P).T
    sm[:, C_GI], sm[:, C_BI] = gsi[ti - 1], bsi[ti - 1]
    sm[:, C_GJ:C_GJ + PB], sm[:, C_GJ + PB] = gsi[tj - 1], 1
    sm[:, C_BJ:C_BJ + PB] = bsi[tj - 1]
    o["small"] = sm
    slot = np.arange(NPROJ)
    x_row = quad == ROW_XV // 32
    o["pair_mask"] = np.concatenate([
        (s[:, :, None] == slot).reshape(P, -1), np.zeros((P, NPROJ)), r[:, None] == slot,
        np.zeros((P, PB)), x_row[:, None]], axis=1).astype(np.float32)
    columns = np.arange(RING)
    o["merge_mask"] = ((r[:, None] - columns) % NPROJ > RING).astype(np.int32)

    wsi = a["L0_rec_Wsi"][row_t - 1]
    o["wsi_rows"] = wsi.T[fld.T]
    first = P * np.arange(TILES)[:, None] // NF
    o["span_mask"] = ((bl - first).T[:, :, None] == np.arange(SPAN)).astype(np.float32)
    o["wsi_small"] = wsi.T
    o["bs_rep"] = np.broadcast_to(a["L0_rec_bs"], (NF, E))

    o["wd_t"] = a["L0_rec_Wd"].T.reshape(2, P, E).transpose(1, 0, 2)
    o["dense_t"] = a["r_dense_t"].T.reshape(2, P, B).transpose(1, 0, 2)
    def rows_of(i, j):
        low, high = np.minimum(i, j), np.maximum(i, j)
        return a["L0_rec_Wl"].T[high * (high - 1) // 2 + low]
    wl = np.zeros((P, KB, L), np.float32)
    pairs = r[:, None] != s
    i, j = np.broadcast_to(ti[:, None], s.shape)[pairs], tj[pairs]
    wl[:, :PB][pairs] = rows_of(i, j)
    wl[x_row, PB] = rows_of(ti[x_row], 0)
    o["wl_blocks"] = wl
    w1 = a["W_top1"]
    o["w1_z"] = w1[:LIVE].reshape(LLIVE, P, H1).transpose(1, 0, 2)
    o["w1_d"] = w1[L:].reshape(2, P, H1).transpose(1, 0, 2)
    o["w2"] = a["W_top2"].reshape(OC1, P, H2).transpose(1, 0, 2)
    return {k: np.ascontiguousarray(v) for k, v in o.items()}


def kernel(**inputs):
    import concourse.bacc as _bacc
    from concourse.bass_utils import run_bass_kernel_spmd as _run

    nc = _bacc.Bacc("TRN2", target_bir_lowering=False, num_devices=1)
    arrays, args = {}, {}
    for name, a in lay_out(inputs).items():
        arrays[f"in_{name}_dram"] = a
        args[name] = nc.dram_tensor(f"in_{name}_dram", a.shape, mybir.dt.from_np(a.dtype), kind="ExternalInput").ap()
    out = nc.dram_tensor("out_0_dram", (B, 1), F32, kind="ExternalOutput").ap()
    dlrm_tower(nc, **args, out=out)
    r = _run(nc, [arrays], core_ids=[0])
    return r.results[0]["out_0_dram"]
```
